# Optimizing a Trainium2 kernel written in Bass

```python
import numpy as np
import jax
import jax.numpy as jnp

def _softmax(x, axis=-1):
    return jax.nn.softmax(x, axis=axis)

def _gelu(x):
    return jax.nn.gelu(x, approximate=True)

def _silu(x):
    return jax.nn.silu(x)

def _sigmoid(x):
    return jax.nn.sigmoid(x)

def _layernorm(x, axis=-1, eps=1e-05):
    m = jnp.mean(x, axis=axis, keepdims=True)
    v = jnp.var(x, axis=axis, keepdims=True)
    return (x - m) / jnp.sqrt(v + eps)

def _scatter_add(tgt, idx, src, axis=0):
    return tgt.at[idx].add(src)

def _segment_sum(src, seg, n):
    return jax.ops.segment_sum(src, seg, n)
kernel_name = 'mk_seq_preln_d1_jaxref_r8_56d71a'

def setup_inputs(seed: int=0):
    np.random.seed(seed)
    _w = jnp.asarray

    def _L0_attn_setup():
        import math
        import jax, jax.numpy as jnp
        import numpy as np
        B, T, H = (2, 256, 128)
        NH, WINDOW = (16, 32)
        HD = H // NH
        key = jax.random.key(seed)
        ks = jax.random.split(key, 4)
        x = jax.random.normal(ks[0], (B, T, H), dtype=jnp.float32)
        W_qkv = jax.random.normal(ks[1], (H, 3 * H), dtype=jnp.float32) * (1.0 / math.sqrt(H))
        b_qkv = jnp.zeros((3 * H,), dtype=jnp.float32)
        W_out = jax.random.normal(ks[2], (H, H), dtype=jnp.float32) * (1.0 / math.sqrt(H))
        b_out = jnp.zeros((H,), dtype=jnp.float32)
        return {'x': x, 'W_qkv': W_qkv, 'b_qkv': b_qkv, 'W_out': W_out, 'b_out': b_out}
    _L0_attn_in = _L0_attn_setup()

    def _L0_ffn_setup():
        import jax, jax.numpy as jnp
        import numpy as np
        DIM = 128
        HID = 512
        E = 8
        TOPK = 2
        ALPHA = 2.0
        B, T = (1, 256)
        DOWN_SCALE = 0.01
        key = jax.random.key(seed)
        ks = jax.random.split(key, 8)
        s = 1.0 / np.sqrt(DIM)
        sh = 1.0 / np.sqrt(HID)
        return {'x': jax.random.normal(ks[0], (B, T, DIM), jnp.float32), 'w_router': jax.random.uniform(ks[1], (DIM, E), jnp.float32, -s, s), 'w_up': jax.random.uniform(ks[2], (E - 1, DIM, HID), jnp.float32, -s, s), 'w_gate': jax.random.uniform(ks[3], (E - 1, DIM, HID), jnp.float32, -s, s), 'w_down': jax.random.normal(ks[4], (E - 1, HID, DIM), jnp.float32) * DOWN_SCALE, 'ws_up': jax.random.uniform(ks[5], (DIM, HID), jnp.float32, -s, s), 'ws_gate': jax.random.uniform(ks[6], (DIM, HID), jnp.float32, -s, s), 'ws_down': jax.random.normal(ks[7], (HID, DIM), jnp.float32) * DOWN_SCALE}
    _L0_ffn_in = _L0_ffn_setup()
    _d = {'L0_attn_x': _L0_attn_in['x'], 'L0_attn_W_qkv': _L0_attn_in['W_qkv'], 'L0_attn_b_qkv': _L0_attn_in['b_qkv'], 'L0_attn_W_out': _L0_attn_in['W_out'], 'L0_attn_b_out': _L0_attn_in['b_out'], 'L0_ffn_w_router': _L0_ffn_in['w_router'], 'L0_ffn_w_up': _L0_ffn_in['w_up'], 'L0_ffn_w_gate': _L0_ffn_in['w_gate'], 'L0_ffn_w_down': _L0_ffn_in['w_down'], 'L0_ffn_ws_up': _L0_ffn_in['ws_up'], 'L0_ffn_ws_gate': _L0_ffn_in['ws_gate'], 'L0_ffn_ws_down': _L0_ffn_in['ws_down']}
    _x0 = _d['L0_attn_x']
    _d['L0_attn_x'] = jax.random.normal(jax.random.fold_in(jax.random.key(seed), 1), (8, 512, 128), dtype=_x0.dtype)
    del _x0
    return _d

def reference(L0_attn_x, L0_attn_W_qkv, L0_attn_b_qkv, L0_attn_W_out, L0_attn_b_out, L0_ffn_w_router, L0_ffn_w_up, L0_ffn_w_gate, L0_ffn_w_down, L0_ffn_ws_up, L0_ffn_ws_gate, L0_ffn_ws_down):

    def _L0_attn_ref(x, W_qkv, b_qkv, W_out, b_out):
        import math
        import jax, jax.numpy as jnp
        import numpy as np
        B, T, H = (2, 256, 128)
        NH, WINDOW = (16, 32)
        HD = H // NH
        b, t, h = x.shape
        qkv = x @ W_qkv + b_qkv
        qkv = qkv.reshape(b, t, 3, NH, HD)
        qkv = jnp.transpose(qkv, (2, 0, 3, 1, 4))
        q, k, v = (qkv[0], qkv[1], qkv[2])
        scores = jnp.einsum('bnid,bnjd->bnij', q, k) / math.sqrt(HD)
        idx = jnp.arange(t)
        diff = idx[:, None] - idx[None, :]
        mask = (diff < 0) | (diff >= WINDOW)
        scores = jnp.where(mask[None, None], -jnp.inf, scores)
        attn = jax.nn.softmax(scores, axis=-1)
        out = jnp.einsum('bnij,bnjd->bnid', attn, v)
        out = jnp.transpose(out, (0, 2, 1, 3)).reshape(b, t, h)
        return out @ W_out + b_out

    def _L0_ffn_ref(x, w_router, w_up, w_gate, w_down, ws_up, ws_gate, ws_down):
        import jax, jax.numpy as jnp
        import numpy as np
        DIM = 128
        HID = 512
        E = 8
        TOPK = 2
        ALPHA = 2.0
        B, T = (1, 256)
        DOWN_SCALE = 0.01
        logits = x @ w_router
        probs = jax.nn.softmax(logits.astype(jnp.float32), axis=-1).astype(logits.dtype)
        topk_vals, topk_idx = jax.lax.top_k(probs, TOPK)
        up = jnp.einsum('btd,edh->ebth', x, w_up)
        gate = jax.nn.silu(jnp.einsum('btd,edh->ebth', x, w_gate))
        exp_out = jnp.einsum('ebth,ehd->ebtd', up * gate, w_down)
        out = jnp.zeros_like(x)
        eids = jnp.arange(E - 1)
        for i in range(TOPK - 1):
            idx_i = topk_idx[..., i]
            sel = (idx_i[None, :, :] == eids[:, None, None]).astype(x.dtype)
            gathered = jnp.einsum('ebt,ebtd->btd', sel, exp_out)
            out = out + ALPHA * topk_vals[..., i:i + 1] * gathered
        shared = x @ ws_up * jax.nn.silu(x @ ws_gate) @ ws_down
        return out + shared
    x = L0_attn_x
    x = x + _L0_attn_ref(_layernorm(x, axis=-1), L0_attn_W_qkv, L0_attn_b_qkv, L0_attn_W_out, L0_attn_b_out)
    x = x + _L0_ffn_ref(_layernorm(x, axis=-1), L0_ffn_w_router, L0_ffn_w_up, L0_ffn_w_gate, L0_ffn_w_down, L0_ffn_ws_up, L0_ffn_ws_gate, L0_ffn_ws_down)
    return x

_drawn_inputs = setup_inputs


def setup_inputs(seed=0):
    import zlib

    import numpy as np

    out = dict(_drawn_inputs(seed))
    spreads = {'L0_attn_b_qkv': (0.0, 0.1), 'L0_attn_b_out': (0.0, 0.1)}
    factors = {'L0_ffn_w_router': 3.015,
     'L0_ffn_w_up': 2.869,
     'L0_ffn_w_gate': 2.977,
     'L0_ffn_w_down': 2.875}
    for name, (base, spread) in spreads.items():
        noise = np.random.default_rng([zlib.crc32(name.encode()), seed]).standard_normal(out[name].shape)
        drawn = base * np.exp(spread * noise) if base else spread * noise
        out[name] = jnp.asarray(drawn.astype(out[name].dtype))
    for name, factor in factors.items():
        out[name] = (out[name] * factor).astype(out[name].dtype)
    return out
```

```python
import math
from contextlib import ExitStack

import concourse.bass as bass
from concourse import mybir


def windowed_attention_top1_moe_kernel(
    nc, x, w_qkv, b_qkv, w_out, b_out, w_router, w_up, w_gate, w_down, ws_up, ws_gate, ws_down, out
):
    f32, bf16 = mybir.dt.float32, mybir.dt.bfloat16
    i32, u32 = mybir.dt.int32, mybir.dt.uint32
    ALU = mybir.AluOpType
    ACT = mybir.ActivationFunctionType
    AX = mybir.AxisListType

    B, T, D = x.shape
    P = 128
    NH, HD, WIN = 16, 8, 32
    BLK = 32
    NJ = P // BLK
    KEYS = 2 * BLK
    HPB = 512 // KEYS
    HPG = BLK // HD
    NG = NH // HPG
    TPB = T // P
    NT = B * TPB
    E = w_router.shape[1]
    NE = E - 1
    HID = w_up.shape[2]
    NC = HID // P
    SHARED = NE
    MT = (NT * P - E) // P + E
    GATE, TOKEN = D, D + 1
    ROW = D + 4
    RING = 4
    NOBODY = 2.0 * NT * P
    ALPHA, EPS = 2.0, 1e-5
    MASKED = -1e30
    SCALE = 1.0 / math.sqrt(HD)
    VW = HD + 1

    ctx = ExitStack()
    with ctx:

        def sb(name, shape, dt=f32):
            return ctx.enter_context(nc.sbuf_tensor(name, shape, dt))

        def sem(name):
            return ctx.enter_context(nc.semaphore(name))

        wqkv_sb = sb("wqkv_sb", [P, 3 * D])
        bqkv_sb = sb("bqkv_sb", [P, 3])
        wout_sb = sb("wout_sb", [P, D])
        bout_sb = sb("bout_sb", [1, D])
        wr_sb = sb("wr_sb", [P, E])
        up_sb = sb("up_sb", [P, E, HID])
        gate_sb = sb("gate_sb", [P, E, HID])
        down_sb = sb("down_sb", [P, E, NC * D])
        ones = sb("ones", [P, NT * E])
        ident = sb("ident", [P, P])
        ident_h = sb("ident_h", [P, P], bf16)
        ones_h = sb("ones_h", [P, P], bf16)
        before_h = sb("before_h", [P, P], bf16)
        mask_h = sb("mask_h", [P, 2, HPB, KEYS], bf16)
        head_of = sb("head_of", [P, HPG])
        bk_of = sb("bk_of", [P, HPG])
        bv_wide = sb("bv_wide", [P, P])
        attn_bias = sb("attn_bias", [P, 1, D])
        x_all = sb("x_all", [P, NT, D])
        stats = sb("stats", [P, NT, 6])
        ln_a = sb("ln_a", [P, NT])
        ln_b = sb("ln_b", [P, NT])
        ln_ve = sb("ln_ve", [P, NT])
        ln_sd = sb("ln_sd", [P, NT])
        mean = sb("mean", [P, NT])
        rstd = sb("rstd", [P, NT])
        xn = sb("xn", [P, TPB, D])
        xnT = sb("xnT", [P, BLK + T])
        Qx = sb("Qx", [P, NG, T])
        Kx = sb("Kx", [P, HPG, BLK + T])
        VD = sb("VD", [P, TPB, 2, NH, NJ, VW])
        row_max = sb("row_max", [P, 2, NH])
        Sd = sb("Sd", [P, 2, NH, KEYS])
        Pr = sb("Pr", [P, 2, NH * KEYS])
        PT = sb("PT", [P, 2, NH * KEYS])
        rden = sb("rden", [P, 2, NH])
        On = sb("On", [P, 2, D])
        OT = sb("OT", [P, 2, D])

        xn2T = sb("xn2T", [P, NT * P])
        rows = sb("rows", [P, NT, ROW])
        top = sb("top", [P, NT])
        chosen = sb("chosen", [P, NT, E])
        best = sb("best", [P, NT])
        chosen_h = sb("chosen_h", [P, E, NT], bf16)
        logit_d = sb("logit_d", [P, NT, E])
        logit_e = sb("logit_e", [P, NT, E])
        esum = sb("esum", [P, NT])
        has_expert = sb("has_expert", [P, NT])
        rank_of = sb("rank_of", [P, E])
        tile_no = sb("tile_no", [P, MT])
        row_no = sb("row_no", [P, NT])
        seen = sb("seen", [P, E, NT])
        count = sb("count", [P, E])
        full = sb("full", [P, E, NT])
        tiles_of = sb("tiles_of", [P, E])
        tiles_end = sb("tiles_end", [P, E])
        shift = sb("shift", [P, E])
        pos3 = sb("pos3", [P, E, NT])
        pos = sb("pos", [P, NT])
        pos_u = sb("pos_u", [P, NT], u32)
        past = sb("past", [P, MT, NE])
        tile_e = sb("tile_e", [P, MT])
        tile_at = sb("tile_at", [P, MT], i32)
        pad_row = sb("pad_row", [P, 1, ROW])
        sg = sb("sg", [P, 2, HID])
        hT = sb("hT", [P, NC, T])
        xs = sb("xs", [P, RING, ROW])
        base = sb("base", [P, RING, D])
        tok_u = sb("tok_u", [P, RING], u32)
        xsT = sb("xsT", [P, 2, P])
        hs = sb("hs", [P, 2, HID])
        hsT = sb("hsT", [P, 2, HID])
        y = sb("y", [P, RING, D])
        sorted_x = nc.dram_tensor("sorted_x", [MT * P, ROW], f32, kind="Internal").ap()
        sorted_base = nc.dram_tensor("sorted_base", [MT * P, D], f32, kind="Internal").ap()

        psS = ctx.enter_context(nc.psum_tensor("psS", [P, 2, 1024], f32))
        psO = ctx.enter_context(nc.psum_tensor("psO", [P, 2, 512], f32))
        psA = ctx.enter_context(nc.psum_tensor("psA", [P, 512], f32))
        psB = ctx.enter_context(nc.psum_tensor("psB", [P, 512], f32))
        OPC = 256

        x_in = [sem(f"x_in{b}") for b in range(B)]
        wqkv_in, bqkv_in = sem("wqkv_in"), sem("bqkv_in")
        wout_in, bout_in = sem("wout_in"), sem("bout_in")
        filled, consts_ready, bv_wide_ready = sem("filled"), sem("consts_ready"), sem("bv_wide_ready")
        bias_mm, bias_ready = sem("bias_mm"), sem("bias_ready")
        zeros_ready, head_of_ready, bk_of_ready = sem("zeros_ready"), sem("head_of_ready"), sem("bk_of_ready")
        ln_step, ln_sd_ready, stats1_done = sem("ln_step"), sem("ln_sd_ready"), sem("stats1_done")
        ln_ve_ready = sem("ln_ve_ready")
        norm_done, xt_done, xnT_ready = sem("norm_done"), sem("xt_done"), sem("xnT_ready")
        qk_done, q_ready, k_ready = sem("qk_done"), sem("q_ready"), sem("k_ready")
        v_done, v_ready = sem("v_done"), sem("v_ready")
        s_done, max_done, sub_done = sem("s_done"), sem("max_done"), sem("sub_done")
        exp_done, pt_done, pv_done = sem("exp_done"), sem("pt_done"), sem("pv_done")
        rden_done, on_done, ot_done = sem("rden_done"), sem("on_done"), sem("ot_done")
        op_done = sem("op_done")
        o_free = sem("o_free")
        xb_done, st2_done = sem("xb_done"), sem("st2_done")
        wr_in, shared_in, experts_in = sem("wr_in"), [sem(f"shared_in{n}") for n in range(3)], [
            sem(f"experts_in{n}") for n in range(3)
        ]
        pads_x, pads_base, pad_ready, rows_turned = sem("pads_x"), sem("pads_base"), sem("pad_ready"), sem("rows_turned")
        rows_ready, xn2T_ready, logits_done = sem("rows_ready"), sem("xn2T_ready"), sem("logits_done")
        logit_d_ready, logit_e_ready = sem("logit_d_ready"), sem("logit_e_ready")
        chosen_ready, counted, gates_ready, pos_ready = (
            sem("chosen_ready"), sem("counted"), sem("gates_ready"), sem("pos_ready"),
        )
        tile_at_ready = sem("tile_at_ready")
        x_scattered, base_scattered = sem("x_scattered"), sem("base_scattered")
        g_done, u_done, silu_done, h_done, down_done, base_done = (
            sem("g_done"), sem("u_done"), sem("silu_done"), sem("h_done"), sem("down_done"), sem("base_done"),
        )
        xs_in = [sem(f"xs_in{r}") for r in range(RING)]
        base_in = [sem(f"base_in{r}") for r in range(RING)]
        written = [sem(f"written{r}") for r in range(RING)]
        tok_ready, xsT_done, xsT_ready = sem("tok_ready"), sem("xsT_done"), sem("xsT_ready")
        eg_done, eu_done, esilu_done, eh_done = sem("eg_done"), sem("eu_done"), sem("esilu_done"), sem("eh_done")
        ehT_done, ehT_ready = sem("ehT_done"), sem("ehT_ready")
        ey_done, y_ready = sem("ey_done"), sem("y_ready")

        def loads(i, r):
            q = r % RING
            return 16 * (i // RING + 1) if isinstance(i, int) else i * (16 // RING) + (16 - (16 // RING) * q)

        x_rows = x.rearrange("b (k p) d -> p (b k) d", p=P)
        out_rows = out.rearrange("b (k p) d -> p (b k) d", p=P)

        block = ctx.enter_context(nc.Block())

        @block.sync
        def _(sp):
            for b in range(B):
                sp.dma_start(x_all[:, b * TPB : (b + 1) * TPB, :], x_rows[:, b * TPB : (b + 1) * TPB, :]).then_inc(
                    x_in[b], 16
                )

            sp.wait_ge(pad_ready, 1)
            sp.dma_start(
                sorted_x.rearrange("(i p) r -> p i r", p=P), pad_row[:, :, :].to_broadcast([P, MT, ROW])
            ).then_inc(pads_x, 16)
            sp.dma_start(
                sorted_base.rearrange("(i p) r -> p i r", p=P), pad_row[:, :, 0:D].to_broadcast([P, MT, D])
            ).then_inc(pads_base, 16)

            def load(i, r, wait=True):
                if wait:
                    sp.wait_ge(eh_done, i - (RING - 1))
                sp.dma_start(xs[:, r, :], sorted_x[bass.ds(i * P, P), :]).then_inc(xs_in[r], 16)

            def load_base(i, r, wait=True):
                if wait:
                    sp.wait_ge(y_ready, i - (RING - 1))
                sp.dma_start(base[:, r, :], sorted_base[bass.ds(i * P, P), :]).then_inc(base_in[r], 16)

            sp.wait_ge(x_scattered, 16 * NT)
            for i in range(RING):
                load(i, i, wait=False)
            sp.wait_ge(base_scattered, 16 * NT)
            for i in range(RING):
                load_base(i, i, wait=False)
            with sp.Fori(RING, MT - MT % RING - RING + 1, RING) as i:
                for r in range(RING):
                    load(i + r, r)
                    load_base(i + r, r)
            for i in range(MT - MT % RING, MT):
                load(i, i % RING)
                load_base(i, i % RING)

        @block.gpsimd
        def _(pool):
            made = [0]

            def make(ins):
                made[0] += 1
                ins.then_inc(filled, 1)
                pool.wait_ge(filled, made[0])

            make(pool.memset(ones[:, :], 1.0))
            make(pool.memset(ident[:, :], 0.0))
            make(pool.affine_select(
                out=ident[:, :], in_=ident[:, :], compare_op=ALU.not_equal, fill=1.0,
                base=0, pattern=[[-1, P]], channel_multiplier=1,
            ))
            make(pool.tensor_copy(ident_h[:, :], ident[:, :]))
            make(pool.memset(Qx[:, :, :], 0.0))
            make(pool.memset(VD[:, :, :, :, :, :], 0.0))
            make(pool.memset(mask_h[:, :, :, :], 0.0))
            for j in range(NJ):
                r = slice(j * BLK, (j + 1) * BLK)
                make(pool.memset(VD[r, :, :, :, j, HD].rearrange("k t c h -> k (t c h)"), 1.0))
                m = mask_h[r, :, :, :].rearrange("q a h k -> q (a h) k")
                make(pool.affine_select(
                    out=m, in_=m, compare_op=ALU.is_ge, fill=MASKED,
                    base=BLK, pattern=[[0, 2 * HPB], [-1, KEYS]], channel_multiplier=1,
                ))
                make(pool.affine_select(
                    out=m, in_=m, compare_op=ALU.is_ge, fill=MASKED,
                    base=WIN - BLK - 1, pattern=[[0, 2 * HPB], [1, KEYS]], channel_multiplier=-1,
                ))
            make(pool.memset(mask_h[0:BLK, 0, :, 0:BLK], MASKED))
            make(pool.memset(ones_h[:, :], 1.0))
            pool.affine_select(
                out=before_h[:, :], in_=ones_h[:, :], compare_op=ALU.is_gt, fill=0.0,
                base=0, pattern=[[1, P]], channel_multiplier=-1,
            ).then_inc(consts_ready, 1)
            make(pool.memset(pad_row[:, :, 0:TOKEN], 0.0))
            pool.memset(pad_row[:, :, TOKEN:], NOBODY).then_inc(pad_ready, 1)
            made_up_to = dict(channel_multiplier=0, allow_small_or_imprecise_dtypes=True)
            make(pool.iota(rank_of[:, :], [[-1, E]], base=E, **made_up_to))
            make(pool.iota(tile_no[:, :], [[1, MT]], base=0, **made_up_to))
            make(pool.iota(row_no[:, :], [[P, NT]], base=0, **made_up_to))
            make(pool.memset(rows[:, :, TOKEN + 1 :], 0.0))
            pool.iota(
                rows[:, :, TOKEN : TOKEN + 1], [[P, NT], [0, 1]], base=0, channel_multiplier=1,
                allow_small_or_imprecise_dtypes=True,
            ).then_inc(consts_ready, 1)

            def add_bias(b):
                pool.wait_ge(norm_done, b + 1)
                xb = x_all[:, bass.ds(b * TPB, TPB), :]
                pool.tensor_tensor(xb, xb, attn_bias[:, :, :].to_broadcast([P, TPB, D]), ALU.add).then_inc(xb_done, 1)

            pool.wait_ge(bias_ready, 1)
            with pool.Fori(0, B) as b:
                add_bias(b)

            pool.wait_ge(pads_x, 16)
            pool.wait_ge(pads_base, 16)
            pool.wait_ge(pos_ready, 1)
            pool.wait_ge(gates_ready, 1)
            for g in range(NT):
                pool.indirect_dma_start(
                    out=sorted_x, out_offset=bass.IndirectOffsetOnAxis(pos_u[:, g : g + 1], 0),
                    in_=rows[:, g, :], in_offset=None,
                ).then_inc(x_scattered, 16)
            for g in range(NT):
                if g % TPB == 0:
                    pool.wait_ge(base_done, g // TPB + 1)
                pool.indirect_dma_start(
                    out=sorted_base, out_offset=bass.IndirectOffsetOnAxis(pos_u[:, g : g + 1], 0),
                    in_=x_all[:, g, :], in_offset=None,
                ).then_inc(base_scattered, 16)

            last_token = pool.to_reg(NT * P - 1)
            out_list = out.rearrange("b t d -> (b t) d")

            def write(i, r):
                pool.wait_ge(y_ready, i + 1)
                pool.indirect_dma_start(
                    out=out_list, out_offset=bass.IndirectOffsetOnAxis(tok_u[:, r : r + 1], 0),
                    in_=y[:, r, :], in_offset=None, bounds_check=last_token, oob_is_err=False,
                ).then_inc(written[r], 16)

            for i in range(MT):
                write(i, i % RING)
            for r in range(RING):
                pool.wait_ge(written[r], 16 * ((MT - 1 - r) // RING + 1))

        @block.scalar
        def _(act):
            act.dma_start(wqkv_sb[:, :], w_qkv).then_inc(wqkv_in, 16)
            act.dma_start(bqkv_sb[:, :], b_qkv.rearrange("(t p) -> p t", p=P), allow_slow_non_contiguous=True).then_inc(bqkv_in, 16)
            act.dma_start(wout_sb[:, :], w_out).then_inc(wout_in, 16)
            act.dma_start(bout_sb[:, :], b_out.rearrange("(a n) -> a n", a=1)).then_inc(bout_in, 16)
            act.dma_start(wr_sb[:, :], w_router).then_inc(wr_in, 16)
            act.dma_start(up_sb[:, SHARED, :], ws_up).then_inc(shared_in[0], 16)
            act.dma_start(gate_sb[:, SHARED, :], ws_gate).then_inc(shared_in[1], 16)
            act.dma_start(
                down_sb[:, SHARED, :].rearrange("p (c d) -> p c d", d=D), ws_down.rearrange("(c p) d -> p c d", p=P)
            ).then_inc(shared_in[2], 16)
            act.dma_start(up_sb[:, 0:NE, :], w_up.rearrange("e p h -> p e h")).then_inc(experts_in[0], 16)
            act.dma_start(gate_sb[:, 0:NE, :], w_gate.rearrange("e p h -> p e h")).then_inc(experts_in[1], 16)
            act.dma_start(
                down_sb[:, 0:NE, :].rearrange("p e (c d) -> p (e c) d", d=D),
                w_down.rearrange("e (c p) d -> p (e c) d", p=P),
            ).then_inc(experts_in[2], 16)
            act.wait_ge(ln_ve_ready, 1)
            nc.scalar.activation(ln_sd[:, :], ln_ve[:, :], ACT.Sqrt).then_inc(ln_sd_ready, 1)

            def evict_xnT(n):
                act.wait_ge(xt_done, n)
                nc.scalar.copy(xnT[:, BLK:], psA[:, :]).then_inc(xnT_ready, 1)

            def evict_qk(n):
                act.wait_ge(qk_done, 2 * n - 1)
                for g in range(NG):
                    r = slice(g * BLK, (g + 1) * BLK)
                    last = nc.scalar.activation(Qx[r, g, :], psA[r, :], ACT.Identity, bias=bqkv_sb[r, 0:1])
                last.then_inc(q_ready, 1)
                act.wait_ge(qk_done, 2 * n)
                for h in range(HPG):
                    last = nc.scalar.activation(
                        Kx[:, h, BLK:], psB[:, :], ACT.Identity, bias=bk_of[:, h : h + 1], scale=head_of[:, h : h + 1]
                    )
                last.then_inc(k_ready, 1)

            def evict_v(n, half, bank):
                act.wait_ge(v_done, 2 * n - 1 + half)
                for j in range(NJ):
                    r = slice(j * BLK, (j + 1) * BLK)
                    dst = VD[r, 2 * half : 2 * half + 2, :, :, j, 0:HD].rearrange("k t c h d -> k (t c) h d")
                    src = bank[r, :].rearrange("k (t h d) -> k t h d", t=4, d=HD)
                    last = nc.scalar.copy(dst, src)
                    last.then_inc(v_ready, 1)

            def exponentials(b, k):
                act.wait_ge(sub_done, b * TPB + (k + 1))
                if k >= 2:
                    act.wait_ge(pt_done, b * TPB + (k - 1))
                nc.scalar.activation(
                    Pr[:, k % 2, :], Sd[:, k % 2, :, :].rearrange("q h k -> q (h k)"), ACT.Exp, scale=SCALE
                ).then_inc(exp_done, 1)

            act.wait_ge(bqkv_in, 16)
            evict_xnT(1)
            act.wait_ge(filled, 5)
            act.wait_ge(bk_of_ready, 1)
            evict_qk(1)
            act.wait_ge(filled, 6)
            evict_v(1, 0, psA)
            evict_v(1, 1, psB)

            def batch(b, more):
                exponentials(b, 0)
                exponentials(b, 1)
                if more:
                    evict_xnT(b + 2)
                exponentials(b, 2)
                exponentials(b, 3)
                if more:
                    evict_qk(b + 2)
                    evict_v(b + 2, 0, psA)
                    evict_v(b + 2, 1, psB)

            with act.Fori(0, B - 1) as b:
                batch(b, True)
            batch(B - 1, False)

            act.wait_ge(ln_ve_ready, 2)
            nc.scalar.activation(ln_sd[:, :], ln_ve[:, :], ACT.Sqrt).then_inc(ln_sd_ready, 1)
            for b in range(B):
                act.wait_ge(rows_turned, b + 1)
                bank = psS[:, b // 2 % 2, 512 * (b % 2) : 512 * (b % 2 + 1)]
                nc.scalar.copy(xn2T[:, b * T : (b + 1) * T], bank).then_inc(xn2T_ready, 1)
            act.wait_ge(logit_d_ready, 1)
            nc.scalar.activation(logit_e[:, :, :], logit_d[:, :, :], ACT.Exp).then_inc(logit_e_ready, 1)

            def shared_silu(b, first=False):
                for c in range(NC):
                    act.wait_ge(g_done, b * NC + (c + 1))
                    if c >= 2 or not first:
                        act.wait_ge(h_done, b * NC + (c - 1))
                    nc.scalar.activation(sg[:, c % 2, :], psS[:, c % 2, 512:], ACT.Silu).then_inc(silu_done, 1)

            shared_silu(0, first=True)
            with act.Fori(1, B) as b:
                shared_silu(b)

            def turned_rows(i, r):
                act.wait_ge(xsT_done, i + 1)
                nc.scalar.copy(xsT[:, r % 2, :], psA[:, 0:P]).then_inc(xsT_ready, 1)

            def expert_step(s, r, ug=True, ht=True, xt=True):
                if xt:
                    turned_rows(s + 1, r + 1)
                if ug:
                    act.wait_ge(eg_done, s + 1)
                    if r >= 2:
                        act.wait_ge(eh_done, s - 1)
                    nc.scalar.activation(sg[:, r % 2, :], psS[:, r % 2, 512:], ACT.Silu).then_inc(esilu_done, 1)
                if ht:
                    act.wait_ge(ehT_done, s)
                    nc.scalar.copy(hsT[:, (r + 1) % 2, :], psO[:, (r + 1) % 2, :]).then_inc(ehT_ready, 1)

            turned_rows(0, 0)
            expert_step(0, 0, ht=False)
            for s in range(1, RING + 2):
                expert_step(s, s)
            with act.Fori(RING + 2, MT - RING, RING) as s:
                for r in range(RING):
                    expert_step(s + r, 2 + r)
            expert_step(MT - 1, MT - 1, xt=False)
            expert_step(MT, MT, ug=False, xt=False)

        @block.vector
        def _(dve):
            step = [0]

            def then(ins):
                step[0] += 1
                ins.then_inc(ln_step, 1)
                dve.wait_ge(ln_step, step[0])

            def ln_moments():
                half = 0.5
                me, mo = stats[:, :, 1], stats[:, :, 4]
                then(nc.vector.tensor_tensor(ln_a[:, :], me, mo, ALU.subtract))
                then(nc.vector.tensor_tensor(mean[:, :], me, mo, ALU.add))
                then(nc.vector.tensor_scalar(mean[:, :], mean[:, :], half, None, ALU.mult))
                then(nc.vector.tensor_tensor(ln_a[:, :], ln_a[:, :], ln_a[:, :], ALU.mult))
                then(nc.vector.tensor_scalar(ln_a[:, :], ln_a[:, :], half * half, EPS, ALU.mult, ALU.add))
                then(nc.vector.tensor_tensor(ln_b[:, :], stats[:, :, 2], stats[:, :, 5], ALU.add))
                nc.vector.scalar_tensor_tensor(
                    out=ln_ve[:, :], in0=ln_b[:, :], scalar=1.0 / D, in1=ln_a[:, :], op0=ALU.mult, op1=ALU.add
                ).then_inc(ln_ve_ready, 1)

            def ln_rstd(n):
                dve.wait_ge(ln_ve_ready, n)
                dve.wait_ge(ln_sd_ready, n)
                then(nc.vector.reciprocal(rstd[:, :], ln_sd[:, :]))
                then(nc.vector.tensor_tensor(ln_a[:, :], rstd[:, :], rstd[:, :], ALU.mult))
                then(nc.vector.tensor_tensor(ln_a[:, :], ln_a[:, :], ln_ve[:, :], ALU.mult))
                then(nc.vector.tensor_scalar(ln_a[:, :], ln_a[:, :], -0.5, 1.5, ALU.mult, ALU.add))
                then(nc.vector.tensor_tensor(rstd[:, :], rstd[:, :], ln_a[:, :], ALU.mult))

            nc.vector.memset(xnT[:, 0:BLK], 0.0)
            nc.vector.memset(Kx[:, :, 0:BLK], 0.0).then_inc(zeros_ready, 1)
            for b in range(B):
                dve.wait_ge(x_in[b], 16)
                for g in range(b * TPB, (b + 1) * TPB):
                    last = nc.vector.bn_stats(stats[:, g, :], x_all[:, g, :])
            last.then_inc(stats1_done, 1)
            dve.wait_ge(stats1_done, 1)
            ln_moments()
            dve.wait_ge(filled, 1)
            dve.wait_ge(bqkv_in, 16)
            nc.vector.tensor_scalar(bv_wide[:, :], ones[:, 0:P], bqkv_sb[:, 2:3], None, ALU.mult).then_inc(
                bv_wide_ready, 1
            )
            dve.wait_ge(filled, 3)
            nc.vector.tensor_reduce(
                head_of[:, :], ident[:, :].rearrange("p (g h d) -> p h g d", g=NG, d=HD), AX.XY, ALU.add
            ).then_inc(head_of_ready, 1)
            dve.wait_ge(head_of_ready, 1)
            nc.vector.tensor_scalar(bk_of[:, :], head_of[:, :], bqkv_sb[:, 1:2], None, ALU.mult).then_inc(bk_of_ready, 1)
            ln_rstd(1)
            dve.wait_ge(bias_mm, 1)
            nc.vector.tensor_copy(attn_bias[:, 0, :], psO[:, 0, 0:D]).then_inc(bias_ready, 1)
            dve.wait_ge(bias_ready, 1)
            for _ in range(2):
                nc.vector.memset(ln_b[:, 0:1], 0.0).then_inc(o_free, 1)
                dve.wait_ge(o_free, 1 + _)

            def normalise(b, wait=True):
                if wait:
                    dve.wait_ge(xt_done, b)
                for k in range(TPB):
                    at = bass.ds(b * TPB + k, 1)
                    last = nc.vector.tensor_scalar(
                        xn[:, k : k + 1, :], x_all[:, at, :], mean[:, at], rstd[:, at], ALU.subtract, ALU.mult
                    )
                last.then_inc(norm_done, 1)

            def softmax(b, k):
                n = b * TPB
                s = psS[:, k % 2, :].rearrange("q (h k) -> q h k", k=KEYS)
                dve.wait_ge(s_done, n + (k + 1))
                nc.vector.tensor_reduce(row_max[:, k % 2, :], s, AX.X, ALU.max).then_inc(max_done, 1)
                dve.wait_ge(max_done, n + (k + 1))
                if k >= 2:
                    dve.wait_ge(exp_done, n + (k - 1))
                nc.vector.tensor_tensor(
                    Sd[:, k % 2, :, :], s, row_max[:, k % 2, :].unsqueeze(2).to_broadcast([P, NH, KEYS]), ALU.subtract
                ).then_inc(sub_done, 1)

            def turn_probs(b, k):
                n = b * TPB
                dve.wait_ge(exp_done, n + (k + 1))
                if k >= 2:
                    dve.wait_ge(pv_done, n + (k - 1))
                nc.vector.transpose(PT[:, k % 2, :], Pr[:, k % 2, :]).then_inc(pt_done, 1)

            def finish_heads(b, k):
                n = b * TPB
                o = psO[:, k % 2, 0 : NH * VW * NJ // NJ].rearrange("q (h j v) -> q h j v", j=NJ, v=VW)
                dve.wait_ge(pv_done, n + (k + 1))
                r = rden[:, k % 2, :].rearrange("q (h j) -> q h j", j=NJ)
                nc.vector.reciprocal(r, o[:, :, :, HD]).then_inc(rden_done, 1)
                dve.wait_ge(rden_done, n + (k + 1))
                nc.vector.tensor_tensor(
                    On[:, k % 2, :].rearrange("q (j h d) -> q h j d", j=NJ, d=HD),
                    o[:, :, :, 0:HD],
                    r.unsqueeze(3).to_broadcast([P, NH // NJ, NJ, HD]),
                    ALU.mult,
                ).then_inc(on_done, 1)
                dve.wait_ge(on_done, n + (k + 1))
                nc.vector.transpose(OT[:, k % 2, :], On[:, k % 2, :]).then_inc(ot_done, 1)

            def residual(b, k):
                n = b * TPB
                dve.wait_ge(op_done, n + (k + 1))
                dve.wait_ge(xb_done, b + 1)
                at = bass.ds(n + k, 1)
                xk = x_all[:, at, :]
                nc.vector.tensor_tensor(
                    xk, xk, psO[:, k % 2, OPC : OPC + D].unsqueeze(1), ALU.add
                ).then_inc(o_free, 1)
                dve.wait_ge(o_free, n + (2 + k + 1))
                nc.vector.bn_stats(stats[:, at, :].rearrange("p a s -> p (a s)"), xk.rearrange("p a d -> p (a d)")).then_inc(st2_done, 1)

            def batch(b, more):
                if more:
                    normalise(b + 1)
                softmax(b, 0)
                softmax(b, 1)
                turn_probs(b, 0)
                softmax(b, 2)
                turn_probs(b, 1)
                finish_heads(b, 0)
                softmax(b, 3)
                turn_probs(b, 2)
                finish_heads(b, 1)
                residual(b, 0)
                turn_probs(b, 3)
                finish_heads(b, 2)
                residual(b, 1)
                finish_heads(b, 3)
                residual(b, 2)
                residual(b, 3)

            normalise(0, wait=False)
            with dve.Fori(0, B - 1) as b:
                batch(b, True)
            batch(B - 1, False)

            dve.wait_ge(st2_done, NT)
            ln_moments()
            ln_rstd(2)
            dve.wait_ge(consts_ready, 2)
            for b in range(B):
                for g in range(b * TPB, (b + 1) * TPB):
                    last = nc.vector.tensor_scalar(
                        rows[:, g, 0:D], x_all[:, g, :], mean[:, g : g + 1], rstd[:, g : g + 1],
                        ALU.subtract, ALU.mult,
                    )
                last.then_inc(rows_ready, 1)

            logits = psO[:, 0, 0 : NT * E].rearrange("p (g e) -> p g e", e=E)

            def wide(a):
                return a.unsqueeze(2).to_broadcast([P, NT, E])

            dve.wait_ge(logits_done, 1)
            then(nc.vector.tensor_reduce(top[:, :], logits, AX.X, ALU.max))
            nc.vector.tensor_tensor(logit_d[:, :, :], logits, wide(top[:, :]), ALU.subtract).then_inc(logit_d_ready, 1)
            dve.wait_ge(logit_d_ready, 1)
            then(nc.vector.scalar_tensor_tensor(
                out=chosen[:, :, :], in0=logit_d[:, :, :], scalar=0.0,
                in1=rank_of[:, :].unsqueeze(1).to_broadcast([P, NT, E]), op0=ALU.is_ge, op1=ALU.mult,
            ))
            then(nc.vector.tensor_reduce(best[:, :], chosen[:, :, :], AX.X, ALU.max))
            then(nc.vector.tensor_tensor(chosen[:, :, :], chosen[:, :, :], wide(best[:, :]), ALU.is_equal))
            nc.vector.tensor_copy(chosen_h[:, :, :].rearrange("p e g -> p g e"), chosen[:, :, :]).then_inc(chosen_ready, 1)
            then(nc.vector.tensor_scalar(has_expert[:, :], chosen[:, :, NE], -ALPHA, ALPHA, ALU.mult, ALU.add))
            dve.wait_ge(logit_e_ready, 1)
            then(nc.vector.tensor_reduce(esum[:, :], logit_e[:, :, :], AX.X, ALU.add))
            then(nc.vector.reciprocal(esum[:, :], esum[:, :]))
            nc.vector.tensor_tensor(rows[:, :, GATE], esum[:, :], has_expert[:, :], ALU.mult).then_inc(gates_ready, 1)
            within = psA[:, 0 : E * NT].rearrange("p (e g) -> p e g", e=E)
            in_tile = psB[:, 0 : E * NT]
            flat = "p e g -> p (e g)"
            dve.wait_ge(counted, 1)
            then(nc.vector.tensor_tensor_scan(
                seen[:, :, :].rearrange(flat), ones[:, :], in_tile, 0.0, ALU.mult, ALU.add
            ))
            then(nc.vector.tensor_tensor(pos3[:, :, :].rearrange(flat), seen[:, :, :].rearrange(flat), in_tile, ALU.subtract))
            then(nc.vector.tensor_tensor(count[:, :], seen[:, :, NT - 1], pos3[:, :, 0], ALU.subtract))
            then(nc.vector.tensor_tensor(
                full[:, :, :], count[:, :].unsqueeze(2).to_broadcast([P, E, NT]),
                row_no[:, :].unsqueeze(1).to_broadcast([P, E, NT]), ALU.is_gt,
            ))
            then(nc.vector.tensor_reduce(tiles_of[:, :], full[:, :, :], AX.X, ALU.add))
            then(nc.vector.tensor_tensor_scan(tiles_end[:, :], ones[:, 0:E], tiles_of[:, :], 0.0, ALU.mult, ALU.add))
            then(nc.vector.tensor_tensor(shift[:, :], tiles_end[:, :], tiles_of[:, :], ALU.subtract))
            then(nc.vector.scalar_tensor_tensor(
                out=shift[:, :], in0=shift[:, :], scalar=float(P), in1=pos3[:, :, 0], op0=ALU.mult, op1=ALU.subtract
            ))
            then(nc.vector.tensor_tensor(pos3[:, :, :], pos3[:, :, :], within, ALU.add))
            then(nc.vector.tensor_tensor(
                pos3[:, :, :], pos3[:, :, :], shift[:, :].unsqueeze(2).to_broadcast([P, E, NT]), ALU.add
            ))
            then(nc.vector.tensor_tensor(
                pos3[:, :, :], pos3[:, :, :], chosen[:, :, :].rearrange("p g e -> p e g"), ALU.mult
            ))
            then(nc.vector.tensor_reduce(pos[:, :], pos3[:, :, :].rearrange("p e g -> p g e"), AX.X, ALU.add))
            nc.vector.tensor_copy(pos_u[:, :], pos[:, :]).then_inc(pos_ready, 1)
            then(nc.vector.tensor_tensor(
                past[:, :, :], tile_no[:, :].unsqueeze(2).to_broadcast([P, MT, NE]),
                tiles_end[:, 0:NE].unsqueeze(1).to_broadcast([P, MT, NE]), ALU.is_ge,
            ))
            then(nc.vector.tensor_reduce(tile_e[:, :], past[:, :, :], AX.X, ALU.add))
            then(nc.vector.tensor_scalar(
                tile_e[:, :], tile_e[:, :], float(NE - 1), float(HID), ALU.min, ALU.mult
            ))
            nc.vector.tensor_copy(tile_at[:, :], tile_e[:, :]).then_inc(tile_at_ready, 1)

            def shared_hidden(b, c, first=False):
                dve.wait_ge(u_done, b * NC + (c + 1))
                dve.wait_ge(silu_done, b * NC + (c + 1))
                if not first:
                    dve.wait_ge(down_done, b)
                nc.vector.tensor_tensor(hT[:, c, :], psS[:, c % 2, 0:512], sg[:, c % 2, :], ALU.mult).then_inc(h_done, 1)

            def shared_residual(b):
                dve.wait_ge(down_done, b + 1)
                xb = x_all[:, bass.ds(b * TPB, TPB), :].rearrange("p k d -> p (k d)")
                nc.vector.tensor_tensor(xb, xb, psO[:, 1, :], ALU.add).then_inc(base_done, 1)

            for c in range(NC):
                shared_hidden(0, c, first=True)
            with dve.Fori(1, B) as b:
                shared_hidden(b, 0)
                shared_residual(b - 1)
                for c in range(1, NC):
                    shared_hidden(b, c)
            shared_residual(B - 1)

            def expert_step(s, r, ug=True, down=True):
                if ug:
                    q = r % RING
                    dve.wait_ge(xs_in[q], loads(s, r))
                    if r >= RING:
                        dve.wait_ge(written[q], loads(s, r) - 16)
                    nc.vector.tensor_copy(tok_u[:, q : q + 1], xs[:, q, TOKEN : TOKEN + 1]).then_inc(tok_ready, 1)
                    dve.wait_ge(eu_done, s + 1)
                    dve.wait_ge(esilu_done, s + 1)
                    if r >= 2:
                        dve.wait_ge(ehT_done, s - 1)
                    nc.vector.scalar_tensor_tensor(
                        out=hs[:, r % 2, :], in0=psS[:, r % 2, 0:512], scalar=xs[:, q, GATE : GATE + 1],
                        in1=sg[:, r % 2, :], op0=ALU.mult, op1=ALU.mult,
                    ).then_inc(eh_done, 1)
                if down:
                    q = (r - 2) % RING
                    dve.wait_ge(ey_done, s - 1)
                    dve.wait_ge(base_in[q], loads(s - 2, r - 2))
                    nc.vector.tensor_tensor(y[:, q, :], psB[:, 0:D], base[:, q, :], ALU.add).then_inc(y_ready, 1)

            for s in range(RING + 2):
                expert_step(s, s, down=s >= 2)
            with dve.Fori(RING + 2, MT - RING, RING) as s:
                for r in range(RING):
                    expert_step(s + r, RING + 2 + r)
            expert_step(MT - 1, MT - 1)
            expert_step(MT, MT, ug=False)
            expert_step(MT + 1, MT + 1, ug=False)

        @block.tensor
        def _(pe):
            mm = nc.tensor.matmul
            pe.wait_ge(bv_wide_ready, 1)
            pe.wait_ge(wout_in, 16)
            pe.wait_ge(bout_in, 16)
            mm(psO[:, 0, 0:D], bv_wide[:, :], wout_sb[:, :], start=True, stop=False)
            mm(psO[:, 0, 0:D], ones[0:1, 0:P], bout_sb[0:1, :], start=False, stop=True).then_inc(bias_mm, 1)

            def turn_x(n):
                pe.wait_ge(norm_done, n)
                for k in range(TPB):
                    last = nc.tensor.transpose(psA[:, k * P : (k + 1) * P], xn[:, k, :], ident[:, :])
                last.then_inc(xt_done, 1)

            def queries_keys(n):
                pe.wait_ge(xnT_ready, n)
                mm(psA[:, :], wqkv_sb[:, 0:D], xnT[:, BLK:], start=True, stop=True).then_inc(qk_done, 1)
                mm(psB[:, :], wqkv_sb[:, D : 2 * D], xnT[:, BLK:], start=True, stop=True).then_inc(qk_done, 1)

            def values(half, bank):
                for t in range(2):
                    k = 2 * half + t
                    for c in range(2):
                        at = k * P + c * BLK
                        col = (2 * t + c) * D
                        last = mm(bank[:, col : col + D], xnT[:, at : at + P], wqkv_sb[:, 2 * D :], start=True, stop=True)
                last.then_inc(v_done, 1)

            def scores(b, k):
                if k >= 2:
                    pe.wait_ge(sub_done, b * TPB + (k - 1))
                first = 0 if k == 0 else 1
                for half in range(2):
                    s = psS[:, k % 2, 512 * half : 512 * (half + 1)]
                    mm(s, ident_h[:, :], mask_h[:, first, :, :], start=True, stop=False, skip_group_check=True)
                    for gg in range(HPB // HPG):
                        g = half * (HPB // HPG) + gg
                        for j in range(NJ):
                            at = k * P + j * BLK
                            last = mm(
                                s[j * BLK : (j + 1) * BLK, gg * HPG * KEYS : (gg + 1) * HPG * KEYS],
                                Qx[:, g, at : at + BLK], Kx[:, :, at : at + KEYS],
                                start=False, stop=True, skip_group_check=True,
                            )
                last.then_inc(s_done, 1)

            def weigh_values(b, k):
                pe.wait_ge(pt_done, b * TPB + (k + 1))
                pe.wait_ge(o_free, b * TPB + (k + 1))
                for hh in range(NH // NJ):
                    for c in range(2):
                        for g in range(NJ):
                            h = g * (NH // NJ) + hh
                            last = mm(
                                psO[g * BLK : (g + 1) * BLK, k % 2, hh * NJ * VW : (hh + 1) * NJ * VW],
                                PT[:, k % 2, (2 * h + c) * BLK : (2 * h + c + 1) * BLK],
                                VD[:, k, c, h, :, :].rearrange("k j v -> k (j v)"),
                                start=(c == 0), stop=(c == 1),
                            )
                last.then_inc(pv_done, 1)

            def project(b, k):
                pe.wait_ge(ot_done, b * TPB + (k + 1))
                mm(psO[:, k % 2, OPC : OPC + D], OT[:, k % 2, :], wout_sb[:, :], start=True, stop=True).then_inc(
                    op_done, 1
                )

            pe.wait_ge(filled, 4)
            pe.wait_ge(zeros_ready, 1)
            turn_x(1)
            pe.wait_ge(wqkv_in, 16)
            queries_keys(1)
            pe.wait_ge(q_ready, 1)
            values(0, psA)
            pe.wait_ge(k_ready, 1)
            values(1, psB)
            pe.wait_ge(consts_ready, 1)

            def batch(b, more):
                pe.wait_ge(k_ready, b + 1)
                scores(b, 0)
                scores(b, 1)
                if more:
                    pe.wait_ge(v_ready, 2 * NJ * b + (2 * NJ))
                    turn_x(b + 2)
                scores(b, 2)
                if not more:
                    pe.wait_ge(v_ready, 2 * NJ * (b + 1))
                weigh_values(b, 0)
                scores(b, 3)
                weigh_values(b, 1)
                if more:
                    queries_keys(b + 2)
                project(b, 0)
                weigh_values(b, 2)
                project(b, 1)
                weigh_values(b, 3)
                if more:
                    pe.wait_ge(q_ready, b + 2)
                    values(0, psA)
                project(b, 2)
                if more:
                    pe.wait_ge(k_ready, b + 2)
                    values(1, psB)
                project(b, 3)

            with pe.Fori(0, B - 1) as b:
                batch(b, True)
            batch(B - 1, False)

            for b in range(B):
                pe.wait_ge(rows_ready, b + 1)
                if b >= 4:
                    pe.wait_ge(xn2T_ready, b - 3)
                bank = psS[:, b // 2 % 2, 512 * (b % 2) : 512 * (b % 2 + 1)]
                for k in range(TPB):
                    last = nc.tensor.transpose(bank[:, k * P : (k + 1) * P], rows[:, b * TPB + k, 0:D], ident[:, :])
                last.then_inc(rows_turned, 1)
            pe.wait_ge(wr_in, 16)
            for g in range(NT):
                if g % TPB == 0:
                    pe.wait_ge(xn2T_ready, g // TPB + 1)
                last = mm(psO[:, 0, g * E : (g + 1) * E], xn2T[:, g * P : (g + 1) * P], wr_sb[:, :], start=True, stop=True)
            last.then_inc(logits_done, 1)

            def rank_tokens():
                pe.wait_ge(chosen_ready, 1)
                ch = chosen_h[:, :, :].rearrange("p e g -> p (e g)")
                mm(psA[:, 0 : E * NT], before_h[:, :], ch, start=True, stop=True)
                mm(psB[:, 0 : E * NT], ones_h[:, :], ch, start=True, stop=True).then_inc(counted, 1)

            def shared_up(b, c, first=False):
                if c >= 2 or not first:
                    pe.wait_ge(h_done, b * NC + (c - 1))
                xt = xn2T[:, bass.ds(b * T, T)]
                w = slice(c * P, (c + 1) * P)
                mm(psS[:, c % 2, 512:], gate_sb[:, SHARED, w], xt, start=True, stop=True).then_inc(g_done, 1)
                mm(psS[:, c % 2, 0:512], up_sb[:, SHARED, w], xt, start=True, stop=True).then_inc(u_done, 1)

            def shared_down(b, first=False):
                pe.wait_ge(h_done, b * NC + NC)
                if not first:
                    pe.wait_ge(base_done, b)
                for k in range(TPB):
                    for c in range(NC):
                        last = mm(
                            psO[:, 1, k * D : (k + 1) * D], hT[:, c, k * P : (k + 1) * P],
                            down_sb[:, SHARED, c * D : (c + 1) * D], start=(c == 0), stop=(c == NC - 1),
                        )
                last.then_inc(down_done, 1)

            for n in range(3):
                pe.wait_ge(shared_in[n], 16)
            shared_up(0, 0, first=True)
            rank_tokens()
            for c in range(1, NC):
                shared_up(0, c, first=True)
            shared_up(1, 0)
            shared_down(0, first=True)
            for c in range(1, NC):
                shared_up(1, c)
            with pe.Fori(2, B) as b:
                shared_up(b, 0)
                shared_down(b - 1)
                for c in range(1, NC):
                    shared_up(b, c)
            shared_down(B - 1)

            up_flat = up_sb[:, :, :].rearrange("p e h -> p (e h)")
            gate_flat = gate_sb[:, :, :].rearrange("p e h -> p (e h)")
            down_flat = down_sb[:, :, :].rearrange("p e h -> p (e h)")

            def expert_turn_rows(i, r):
                pe.wait_ge(xs_in[r % RING], loads(i, r))
                if r >= 1:
                    pe.wait_ge(xsT_ready, i)
                nc.tensor.transpose(psA[:, 0:P], xs[:, r % RING, 0:D], ident[:, :]).then_inc(xsT_done, 1)

            def weights_of(i):
                return pe.value_load(tile_at[0:1, bass.ds(i, 1)], min_val=0, max_val=(NE - 1) * HID)

            def expert_step(s, r, ug=True, ht=True, xt=True, down=True):
                if xt:
                    expert_turn_rows(s + 1, r + 1)
                if ug:
                    w = bass.ds(weights_of(s), HID)
                    pe.wait_ge(xsT_ready, s + 1)
                    if r >= 2:
                        pe.wait_ge(eh_done, s - 1)
                    mm(psS[:, r % 2, 512:], xsT[:, r % 2, :], gate_flat[:, w], start=True, stop=True).then_inc(eg_done, 1)
                    mm(psS[:, r % 2, 0:512], xsT[:, r % 2, :], up_flat[:, w], start=True, stop=True).then_inc(eu_done, 1)
                if down:
                    at = weights_of(s - 2)
                    pe.wait_ge(ehT_ready, s - 1)
                    if r >= 3:
                        pe.wait_ge(y_ready, s - 2)
                    for c in range(NC):
                        last = mm(
                            psB[:, 0:D], hsT[:, r % 2, c * P : (c + 1) * P], down_flat[:, bass.ds(at + c * D, D)],
                            start=(c == 0), stop=(c == NC - 1),
                        )
                    last.then_inc(ey_done, 1)
                if ht:
                    pe.wait_ge(eh_done, s)
                    for c in range(NC):
                        w = slice(c * P, (c + 1) * P)
                        last = nc.tensor.transpose(psO[:, (r + 1) % 2, w], hs[:, (r + 1) % 2, w], ident[:, :])
                    last.then_inc(ehT_done, 1)

            for n in range(3):
                pe.wait_ge(experts_in[n], 16)
            pe.wait_ge(tile_at_ready, 1)
            expert_turn_rows(0, 0)
            for s in range(RING + 2):
                expert_step(s, s, ht=s >= 1, down=s >= 2)
            with pe.Fori(RING + 2, MT - RING, RING) as s:
                for r in range(RING):
                    expert_step(s + r, RING + 2 + r)
            expert_step(MT - 1, MT - 1, xt=False)
            expert_step(MT, MT, ug=False, xt=False)
            expert_step(MT + 1, MT + 1, ug=False, ht=False, xt=False)


_INS = [
    "L0_attn_x", "L0_attn_W_qkv", "L0_attn_b_qkv", "L0_attn_W_out", "L0_attn_b_out", "L0_ffn_w_router",
    "L0_ffn_w_up", "L0_ffn_w_gate", "L0_ffn_w_down", "L0_ffn_ws_up", "L0_ffn_ws_gate", "L0_ffn_ws_down",
]


def kernel(**inputs):
    import concourse.bacc as bacc
    import numpy as np
    from concourse.bass_utils import run_bass_kernel_spmd

    nc = bacc.Bacc("TRN2", target_bir_lowering=False, num_devices=1)
    arrays, args = {}, []
    for name in _INS:
        a = np.ascontiguousarray(inputs[name])
        arrays[f"in_{name}"] = a
        args.append(nc.dram_tensor(f"in_{name}", a.shape, mybir.dt.from_np(a.dtype), kind="ExternalInput").ap())
    x = arrays["in_L0_attn_x"]
    args.append(nc.dram_tensor("out", x.shape, mybir.dt.from_np(x.dtype), kind="ExternalOutput").ap())
    windowed_attention_top1_moe_kernel(nc, *args)
    return run_bass_kernel_spmd(nc, [arrays], core_ids=[0]).results[0]["out"]
```

```python
import math
from contextlib import ExitStack

import concourse.bass as bass
from concourse import mybir


def windowed_attention_top1_moe_kernel(
    nc, x, w_qkv, b_qkv, w_out, b_out, w_router, w_up, w_gate, w_down, ws_up, ws_gate, ws_down, out
):
    f32, bf16 = mybir.dt.float32, mybir.dt.bfloat16
    i32, u32 = mybir.dt.int32, mybir.dt.uint32
    ALU = mybir.AluOpType
    ACT = mybir.ActivationFunctionType
    AX = mybir.AxisListType

    B, T, D = x.shape
    P = 128
    NH, HD, WIN = 16, 8, 32
    BLK = 32
    NJ = P // BLK
    KEYS = 2 * BLK
    HPB = 512 // KEYS
    HPG = BLK // HD
    NG = NH // HPG
    TPB = T // P
    NT = B * TPB
    E = w_router.shape[1]
    NE = E - 1
    HID = w_up.shape[2]
    NC = HID // P
    SHARED = NE
    MT = (NT * P - E) // P + E
    GATE, TOKEN = D, D + 1
    ROW = D + 4
    LATE = 2
    RING = 4
    NOBODY = 2.0 * NT * P
    ALPHA, EPS = 2.0, 1e-5
    MASKED = -1e30
    SCALE = 1.0 / math.sqrt(HD)
    VW = HD + 1

    ctx = ExitStack()
    with ctx:

        def sb(name, shape, dt=f32):
            return ctx.enter_context(nc.sbuf_tensor(name, shape, dt))

        def sem(name):
            return ctx.enter_context(nc.semaphore(name))

        wqkv_sb = sb("wqkv_sb", [P, 3 * D])
        bqkv_sb = sb("bqkv_sb", [P, 3])
        wout_sb = sb("wout_sb", [P, D])
        bout_sb = sb("bout_sb", [1, D])
        wr_sb = sb("wr_sb", [P, E])
        up_sb = sb("up_sb", [P, E, HID])
        gate_sb = sb("gate_sb", [P, E, HID])
        down_sb = sb("down_sb", [P, E, NC * D])
        ones = sb("ones", [P, NT * E])
        ident = sb("ident", [P, P])
        ident_h = sb("ident_h", [P, P], bf16)
        ones_h = sb("ones_h", [P, P], bf16)
        before_h = sb("before_h", [P, P], bf16)
        mask_h = sb("mask_h", [P, 2, HPB, KEYS], bf16)
        head_of = sb("head_of", [P, HPG])
        bk_of = sb("bk_of", [P, HPG])
        bv_wide = sb("bv_wide", [P, P])
        attn_bias = sb("attn_bias", [P, 1, D])
        rows = sb("rows", [P, NT, 2, ROW])
        x_all = rows[:, :, 1, 0:D]
        stats = sb("stats", [P, NT, 6])
        ln_a = sb("ln_a", [P, NT])
        ln_b = sb("ln_b", [P, NT])
        ln_ve = sb("ln_ve", [P, NT])
        ln_sd = sb("ln_sd", [P, NT])
        mean = sb("mean", [P, NT])
        rstd = sb("rstd", [P, NT])
        xn = sb("xn", [P, TPB, D])
        xnT = sb("xnT", [P, BLK + T])
        Qx = sb("Qx", [P, 2, NG, T])
        Kx = sb("Kx", [P, 2, HPG, BLK + T])
        VD = sb("VD", [P, TPB, 2, NH, NJ, VW])
        row_max = sb("row_max", [P, 2, NH])
        Sd = sb("Sd", [P, 2, NH, KEYS])
        Pr = sb("Pr", [P, 2, NH * KEYS])
        PT = sb("PT", [P, 2, NH * KEYS])
        rden = sb("rden", [P, 2, NH])
        On = sb("On", [P, 2, D])
        OT = sb("OT", [P, 2, D])

        xn2T = sb("xn2T", [P, NT * P])
        top = sb("top", [P, NT])
        chosen = sb("chosen", [P, NT, E])
        best = sb("best", [P, NT])
        chosen_h = sb("chosen_h", [P, E, NT], bf16)
        logit_d = sb("logit_d", [P, NT, E])
        logit_e = sb("logit_e", [P, NT, E])
        esum = sb("esum", [P, NT])
        has_expert = sb("has_expert", [P, NT])
        rank_of = sb("rank_of", [P, E])
        tile_no = sb("tile_no", [P, MT])
        row_no = sb("row_no", [P, NT])
        seen = sb("seen", [P, E, NT])
        count = sb("count", [P, E])
        full = sb("full", [P, E, NT])
        tiles_of = sb("tiles_of", [P, E])
        tiles_end = sb("tiles_end", [P, E])
        shift = sb("shift", [P, E])
        pos3 = sb("pos3", [P, E, NT])
        pos = sb("pos", [P, NT])
        pos_u = sb("pos_u", [P, NT], u32)
        half_pos = sb("half_pos", [P, 2, LATE * TPB])
        half_pos_u = sb("half_pos_u", [P, 2, LATE * TPB], u32)
        past = sb("past", [P, MT, NE])
        tile_e = sb("tile_e", [P, MT])
        tile_at = sb("tile_at", [P, MT], i32)
        pad_row = sb("pad_row", [P, 1, 2 * ROW])
        sg = PT[:, 0, :].rearrange("p (a h) -> p a h", a=2)
        hT = Sd[:, :, :, :].rearrange("p a h k -> p (a h k)").rearrange("p (c t) -> p c t", c=NC)
        xs = sb("xs", [P, RING, ROW])
        base = sb("base", [P, RING, D])
        tok_u = sb("tok_u", [P, RING], u32)
        xsT = sb("xsT", [P, 2, P])
        hs = Pr[:, 0, :].rearrange("p (a h) -> p a h", a=2)
        hsT = Pr[:, 1, :].rearrange("p (a h) -> p a h", a=2)
        y = sb("y", [P, RING, D])
        sorted_rows = nc.dram_tensor("sorted_rows", [MT * P, 2 * ROW], f32, kind="Internal").ap()
        sorted_halves = sorted_rows.rearrange("t (a r) -> (t a) r", a=2)

        psS = ctx.enter_context(nc.psum_tensor("psS", [P, 2, 1024], f32))
        psO = ctx.enter_context(nc.psum_tensor("psO", [P, 2, 512], f32))
        psA = ctx.enter_context(nc.psum_tensor("psA", [P, 512], f32))
        psB = ctx.enter_context(nc.psum_tensor("psB", [P, 512], f32))
        OPC = 256

        x_in = [sem(f"x_in{b}") for b in range(B)]
        wqkv_in, bqkv_in = sem("wqkv_in"), sem("bqkv_in")
        wout_in, bout_in = sem("wout_in"), sem("bout_in")
        filled, consts_ready, bv_wide_ready = sem("filled"), sem("consts_ready"), sem("bv_wide_ready")
        bias_mm, bias_ready = sem("bias_mm"), sem("bias_ready")
        zeros_ready, head_of_ready, bk_of_ready = sem("zeros_ready"), sem("head_of_ready"), sem("bk_of_ready")
        ln_step, ln_sd_ready, stats1_done = sem("ln_step"), sem("ln_sd_ready"), sem("stats1_done")
        rstd_ready, shift_ready = sem("rstd_ready"), sem("shift_ready")
        ln_ve_ready = sem("ln_ve_ready")
        norm_done, xt_done, xnT_ready = sem("norm_done"), sem("xt_done"), sem("xnT_ready")
        qk_done, q_ready, k_ready = sem("qk_done"), sem("q_ready"), sem("k_ready")
        v_done, v_ready = sem("v_done"), sem("v_ready")
        s_done, max_done, sub_done = sem("s_done"), sem("max_done"), sem("sub_done")
        exp_done, pt_done, pv_done = sem("exp_done"), sem("pt_done"), sem("pv_done")
        rden_done, on_done, ot_done = sem("rden_done"), sem("on_done"), sem("ot_done")
        op_done = sem("op_done")
        o_free = sem("o_free")
        xb_done, st2_done = sem("xb_done"), sem("st2_done")
        wr_in, shared_in, experts_in = sem("wr_in"), [sem(f"shared_in{n}") for n in range(3)], [
            sem(f"experts_in{n}") for n in range(3)
        ]
        pads_written, pad_ready, rows_turned = sem("pads_written"), sem("pad_ready"), sem("rows_turned")
        rows_ready, xn2T_ready, logits_done = sem("rows_ready"), sem("xn2T_ready"), sem("logits_done")
        logit_d_ready, logit_e_ready = sem("logit_d_ready"), sem("logit_e_ready")
        chosen_ready, counted, gates_ready, pos_ready = (
            sem("chosen_ready"), sem("counted"), sem("gates_ready"), sem("pos_ready"),
        )
        tile_at_ready = sem("tile_at_ready")
        x_scattered, base_scattered = sem("x_scattered"), sem("base_scattered")
        g_done, u_done, silu_done, h_done, down_done, base_done = (
            sem("g_done"), sem("u_done"), sem("silu_done"), sem("h_done"), sem("down_done"), sem("base_done"),
        )
        xs_in = [sem(f"xs_in{r}") for r in range(RING)]
        base_in = [sem(f"base_in{r}") for r in range(RING)]
        written = [sem(f"written{r}") for r in range(RING)]
        tok_ready, xsT_done, xsT_ready = sem("tok_ready"), sem("xsT_done"), sem("xsT_ready")
        eg_done, eu_done, esilu_done, eh_done = sem("eg_done"), sem("eu_done"), sem("esilu_done"), sem("eh_done")
        ehT_done, ehT_ready = sem("ehT_done"), sem("ehT_ready")
        ey_done, y_ready = sem("ey_done"), sem("y_ready")

        def loads(i, r):
            q = r % RING
            return 16 * (i // RING + 1) if isinstance(i, int) else i * (16 // RING) + (16 - (16 // RING) * q)

        x_rows = x.rearrange("b (k p) d -> p (b k) d", p=P)
        out_rows = out.rearrange("b (k p) d -> p (b k) d", p=P)

        block = ctx.enter_context(nc.Block())

        @block.sync
        def _(sp):
            for b in range(B):
                sp.dma_start(x_all[:, b * TPB : (b + 1) * TPB, :], x_rows[:, b * TPB : (b + 1) * TPB, :]).then_inc(
                    x_in[b], 16
                )

            sp.wait_ge(pad_ready, 1)
            sp.dma_start(
                sorted_rows.rearrange("(i p) r -> p i r", p=P), pad_row[:, :, :].to_broadcast([P, MT, 2 * ROW])
            ).then_inc(pads_written, 16)

            def load(i, r, wait=True):
                if wait:
                    sp.wait_ge(eh_done, i - (RING - 1))
                sp.dma_start(xs[:, r, :], sorted_rows[bass.ds(i * P, P), 0:ROW]).then_inc(xs_in[r], 16)

            def load_base(i, r, wait=True):
                if wait:
                    sp.wait_ge(y_ready, i - (RING - 1))
                sp.dma_start(base[:, r, :], sorted_rows[bass.ds(i * P, P), ROW : ROW + D]).then_inc(base_in[r], 16)

            sp.wait_ge(x_scattered, 16 * NT)
            for i in range(RING):
                load(i, i, wait=False)
            sp.wait_ge(base_scattered, 16 * LATE * TPB)
            for i in range(RING):
                load_base(i, i, wait=False)
            with sp.Fori(RING, MT - MT % RING - RING + 1, RING) as i:
                for r in range(RING):
                    load(i + r, r)
                    load_base(i + r, r)
            for i in range(MT - MT % RING, MT):
                load(i, i % RING)
                load_base(i, i % RING)

        @block.gpsimd
        def _(pool):
            made = [0]

            def make(ins):
                made[0] += 1
                ins.then_inc(filled, 1)
                pool.wait_ge(filled, made[0])

            make(pool.memset(ones[:, :], 1.0))
            make(pool.memset(ident[:, :], 0.0))
            make(pool.affine_select(
                out=ident[:, :], in_=ident[:, :], compare_op=ALU.not_equal, fill=1.0,
                base=0, pattern=[[-1, P]], channel_multiplier=1,
            ))
            make(pool.tensor_copy(ident_h[:, :], ident[:, :]))
            make(pool.memset(Qx[:, :, :, :], 0.0))
            make(pool.memset(VD[:, :, :, :, :, :], 0.0))
            make(pool.memset(mask_h[:, :, :, :], 0.0))
            for j in range(NJ):
                r = slice(j * BLK, (j + 1) * BLK)
                make(pool.memset(VD[r, :, :, :, j, HD].rearrange("k t c h -> k (t c h)"), 1.0))
                m = mask_h[r, :, :, :].rearrange("q a h k -> q (a h) k")
                make(pool.affine_select(
                    out=m, in_=m, compare_op=ALU.is_ge, fill=MASKED,
                    base=BLK, pattern=[[0, 2 * HPB], [-1, KEYS]], channel_multiplier=1,
                ))
                make(pool.affine_select(
                    out=m, in_=m, compare_op=ALU.is_ge, fill=MASKED,
                    base=WIN - BLK - 1, pattern=[[0, 2 * HPB], [1, KEYS]], channel_multiplier=-1,
                ))
            make(pool.memset(mask_h[0:BLK, 0, :, 0:BLK], MASKED))
            make(pool.memset(ones_h[:, :], 1.0))
            pool.affine_select(
                out=before_h[:, :], in_=ones_h[:, :], compare_op=ALU.is_gt, fill=0.0,
                base=0, pattern=[[1, P]], channel_multiplier=-1,
            ).then_inc(consts_ready, 1)
            make(pool.memset(pad_row[:, :, 0:TOKEN], 0.0))
            pool.memset(pad_row[:, :, TOKEN:], NOBODY).then_inc(pad_ready, 1)
            made_up_to = dict(channel_multiplier=0, allow_small_or_imprecise_dtypes=True)
            make(pool.iota(rank_of[:, :], [[-1, E]], base=E, **made_up_to))
            make(pool.iota(tile_no[:, :], [[1, MT]], base=0, **made_up_to))
            make(pool.iota(row_no[:, :], [[P, NT]], base=0, **made_up_to))
            make(pool.memset(rows[:, :, 0, TOKEN + 1 :], 0.0))
            make(pool.memset(rows[:, :, 1, D:], 0.0))
            pool.iota(
                rows[:, :, 0, TOKEN : TOKEN + 1], [[P, NT], [0, 1]], base=0, channel_multiplier=1,
                allow_small_or_imprecise_dtypes=True,
            ).then_inc(consts_ready, 1)

            def add_bias(b):
                pool.wait_ge(norm_done, b + 1)
                xb = x_all[:, bass.ds(b * TPB, TPB), :]
                pool.tensor_tensor(xb, xb, attn_bias[:, :, :].to_broadcast([P, TPB, D]), ALU.add).then_inc(xb_done, 1)

            pool.wait_ge(bias_ready, 1)
            with pool.Fori(0, B) as b:
                add_bias(b)

            def scatter(g):
                pool.indirect_dma_start(
                    out=sorted_rows, out_offset=bass.IndirectOffsetOnAxis(pos_u[:, g : g + 1], 0),
                    in_=rows[:, g, :, :].rearrange("p a r -> p (a r)"), in_offset=None,
                ).then_inc(x_scattered, 16)

            def scatter_half(g, half, done):
                n = g - (B - LATE) * TPB
                pool.indirect_dma_start(
                    out=sorted_halves, out_offset=bass.IndirectOffsetOnAxis(half_pos_u[:, half, n : n + 1], 0),
                    in_=rows[:, g, half, :], in_offset=None,
                ).then_inc(done, 16)

            pool.wait_ge(pads_written, 16)
            pool.wait_ge(gates_ready, 1)
            pool.wait_ge(pos_ready, 1)
            for g in range((B - LATE) * TPB, NT):
                scatter_half(g, 0, x_scattered)
            for g in range(NT):
                if g % TPB == 0:
                    pool.wait_ge(base_done, g // TPB + 1)
                if g < (B - LATE) * TPB:
                    scatter(g)
                else:
                    scatter_half(g, 1, base_scattered)

            last_token = pool.to_reg(NT * P - 1)
            out_list = out.rearrange("b t d -> (b t) d")

            def write(i, r):
                pool.wait_ge(y_ready, i + 1)
                pool.indirect_dma_start(
                    out=out_list, out_offset=bass.IndirectOffsetOnAxis(tok_u[:, r : r + 1], 0),
                    in_=y[:, r, :], in_offset=None, bounds_check=last_token, oob_is_err=False,
                ).then_inc(written[r], 16)

            for i in range(MT):
                write(i, i % RING)
            for r in range(RING):
                pool.wait_ge(written[r], 16 * ((MT - 1 - r) // RING + 1))

        @block.scalar
        def _(act):
            act.dma_start(wqkv_sb[:, :], w_qkv).then_inc(wqkv_in, 16)
            act.dma_start(bqkv_sb[:, :], b_qkv.rearrange("(t p) -> p t", p=P), allow_slow_non_contiguous=True).then_inc(bqkv_in, 16)
            act.dma_start(wout_sb[:, :], w_out).then_inc(wout_in, 16)
            act.dma_start(bout_sb[:, :], b_out.rearrange("(a n) -> a n", a=1)).then_inc(bout_in, 16)
            act.dma_start(wr_sb[:, :], w_router).then_inc(wr_in, 16)
            act.dma_start(up_sb[:, SHARED, :], ws_up).then_inc(shared_in[0], 16)
            act.dma_start(gate_sb[:, SHARED, :], ws_gate).then_inc(shared_in[1], 16)
            act.dma_start(
                down_sb[:, SHARED, :].rearrange("p (c d) -> p c d", d=D), ws_down.rearrange("(c p) d -> p c d", p=P)
            ).then_inc(shared_in[2], 16)
            act.dma_start(up_sb[:, 0:NE, :], w_up.rearrange("e p h -> p e h")).then_inc(experts_in[0], 16)
            act.dma_start(gate_sb[:, 0:NE, :], w_gate.rearrange("e p h -> p e h")).then_inc(experts_in[1], 16)
            act.dma_start(
                down_sb[:, 0:NE, :].rearrange("p e (c d) -> p (e c) d", d=D),
                w_down.rearrange("e (c p) d -> p (e c) d", p=P),
            ).then_inc(experts_in[2], 16)
            act.wait_ge(ln_ve_ready, 1)
            nc.scalar.activation(ln_sd[:, :], ln_ve[:, :], ACT.Sqrt).then_inc(ln_sd_ready, 1)

            def evict_xnT(n, first=False):
                act.wait_ge(xt_done, n)
                if not first:
                    act.wait_ge(v_done, 2 * n - 2)
                nc.scalar.copy(xnT[:, BLK:], psA[:, :]).then_inc(xnT_ready, 1)

            def evict_q(n, odd):
                act.wait_ge(qk_done, 2 * n - 1)
                for g in range(NG):
                    r = slice(g * BLK, (g + 1) * BLK)
                    last = nc.scalar.activation(Qx[r, odd, g, :], psA[r, :], ACT.Identity, bias=bqkv_sb[r, 0:1])
                last.then_inc(q_ready, 1)

            def evict_k(n, odd):
                act.wait_ge(qk_done, 2 * n)
                for h in range(HPG):
                    last = nc.scalar.activation(
                        Kx[:, odd, h, BLK:], psB[:, :], ACT.Identity, bias=bk_of[:, h : h + 1], scale=head_of[:, h : h + 1]
                    )
                last.then_inc(k_ready, 1)

            def evict_v(n, half, bank, first=False):
                act.wait_ge(v_done, 2 * n - 1 + half)
                if not first:
                    act.wait_ge(pv_done, TPB * (n - 2) + 2 * (half + 1))
                for j in range(NJ):
                    r = slice(j * BLK, (j + 1) * BLK)
                    dst = VD[r, 2 * half : 2 * half + 2, :, :, j, 0:HD].rearrange("k t c h d -> k (t c) h d")
                    src = bank[r, :].rearrange("k (t h d) -> k t h d", t=4, d=HD)
                    last = nc.scalar.copy(dst, src)
                    last.then_inc(v_ready, 1)

            def exponentials(b, k, first=False):
                act.wait_ge(sub_done, b * TPB + (k + 1))
                if k >= 2 or not first:
                    act.wait_ge(pt_done, b * TPB + (k - 1))
                nc.scalar.activation(
                    Pr[:, k % 2, :], Sd[:, k % 2, :, :].rearrange("q h k -> q (h k)"), ACT.Exp, scale=SCALE
                ).then_inc(exp_done, 1)

            def normalise(b, first=False):
                if not first:
                    act.wait_ge(xt_done, b)
                for k in range(TPB):
                    at = bass.ds(b * TPB + k, 1)
                    last = nc.scalar.activation(
                        xn[:, k : k + 1, :], x_all[:, at, :], ACT.Identity, bias=ln_b[:, at], scale=rstd[:, at]
                    )
                last.then_inc(norm_done, 1)

            act.wait_ge(bqkv_in, 16)
            act.wait_ge(shift_ready, 1)
            normalise(0, first=True)
            evict_xnT(1, first=True)
            normalise(1)
            act.wait_ge(filled, 5)
            act.wait_ge(bk_of_ready, 1)
            evict_q(1, 0)
            evict_k(1, 0)
            act.wait_ge(filled, 6)
            evict_v(1, 0, psA, first=True)
            exponentials(0, 0, first=True)
            evict_xnT(2)
            evict_v(1, 1, psB, first=True)

            def batch(b, odd, first=False, qkv=True, xt=True):
                if qkv:
                    if not first:
                        act.wait_ge(s_done, b * TPB)
                    evict_q(b + 2, 1 - odd)
                exponentials(b, 1, first=first)
                if qkv:
                    evict_k(b + 2, 1 - odd)
                exponentials(b, 2)
                if xt:
                    normalise(b + 2)
                exponentials(b, 3)
                if qkv:
                    evict_v(b + 2, 0, psA)
                if xt:
                    evict_xnT(b + 3)
                if qkv:
                    exponentials(b + 1, 0)
                    evict_v(b + 2, 1, psB)

            batch(0, 0, first=True)
            with act.Fori(1, B - 3, 2) as b:
                batch(b, 1)
                batch(b + 1, 0)
            batch(B - 3, 1)
            batch(B - 2, 0, xt=False)
            batch(B - 1, 1, qkv=False, xt=False)

            act.wait_ge(ln_ve_ready, 2)
            nc.scalar.activation(ln_sd[:, :], ln_ve[:, :], ACT.Sqrt).then_inc(ln_sd_ready, 1)
            def turned_batch(b):
                act.wait_ge(rows_turned, b + 1)
                nc.scalar.copy(xn2T[:, b * T : (b + 1) * T], (psA, psB)[b % 2][:, :]).then_inc(xn2T_ready, 1)

            def shared_silu(b, c, first=False):
                act.wait_ge(g_done, b * NC + (c + 1))
                if c >= 2 or not first:
                    act.wait_ge(h_done, b * NC + (c - 1))
                nc.scalar.activation(sg[:, c % 2, :], psS[:, c % 2, 512:], ACT.Silu).then_inc(silu_done, 1)

            turned_batch(0)
            turned_batch(1)
            for c in range(NC - 1):
                shared_silu(0, c, first=True)
                turned_batch(2 * c + 2)
                turned_batch(2 * c + 3)
            shared_silu(0, NC - 1)
            shared_silu(1, 0)
            shared_silu(1, 1)
            act.wait_ge(logit_d_ready, 1)
            nc.scalar.activation(logit_e[:, :, :], logit_d[:, :, :], ACT.Exp).then_inc(logit_e_ready, 1)
            shared_silu(1, 2)
            shared_silu(1, 3)
            with act.Fori(2, B) as b:
                for c in range(NC):
                    shared_silu(b, c)

            def turned_rows(i, r):
                act.wait_ge(xsT_done, i + 1)
                nc.scalar.copy(xsT[:, r % 2, :], psA[:, 0:P]).then_inc(xsT_ready, 1)

            def expert_step(s, r, ug=True, ht=True, xt=True):
                if xt:
                    turned_rows(s + 1, r + 1)
                if ug:
                    act.wait_ge(eg_done, s + 1)
                    if r >= 2:
                        act.wait_ge(eh_done, s - 1)
                    nc.scalar.activation(sg[:, r % 2, :], psS[:, r % 2, 512:], ACT.Silu).then_inc(esilu_done, 1)
                if ht:
                    act.wait_ge(ehT_done, s)
                    nc.scalar.copy(hsT[:, (r + 1) % 2, :], psO[:, (r + 1) % 2, :]).then_inc(ehT_ready, 1)

            turned_rows(0, 0)
            expert_step(0, 0, ht=False)
            for s in range(1, RING + 2):
                expert_step(s, s)
            with act.Fori(RING + 2, MT - RING, RING) as s:
                for r in range(RING):
                    expert_step(s + r, 2 + r)
            expert_step(MT - 1, MT - 1, xt=False)
            expert_step(MT, MT, ug=False, xt=False)

        @block.vector
        def _(dve):
            step = [0]

            def then(ins):
                step[0] += 1
                ins.then_inc(ln_step, 1)
                dve.wait_ge(ln_step, step[0])

            def ln_moments():
                half = 0.5
                me, mo = stats[:, :, 1], stats[:, :, 4]
                then(nc.vector.tensor_tensor(ln_a[:, :], me, mo, ALU.subtract))
                then(nc.vector.tensor_tensor(mean[:, :], me, mo, ALU.add))
                then(nc.vector.tensor_scalar(mean[:, :], mean[:, :], half, None, ALU.mult))
                then(nc.vector.tensor_tensor(ln_a[:, :], ln_a[:, :], ln_a[:, :], ALU.mult))
                then(nc.vector.tensor_scalar(ln_a[:, :], ln_a[:, :], half * half, EPS, ALU.mult, ALU.add))
                then(nc.vector.tensor_tensor(ln_b[:, :], stats[:, :, 2], stats[:, :, 5], ALU.add))
                nc.vector.scalar_tensor_tensor(
                    out=ln_ve[:, :], in0=ln_b[:, :], scalar=1.0 / D, in1=ln_a[:, :], op0=ALU.mult, op1=ALU.add
                ).then_inc(ln_ve_ready, 1)

            def ln_rstd(n):
                dve.wait_ge(ln_ve_ready, n)
                dve.wait_ge(ln_sd_ready, n)
                then(nc.vector.reciprocal(rstd[:, :], ln_sd[:, :]))
                then(nc.vector.tensor_tensor(ln_a[:, :], rstd[:, :], rstd[:, :], ALU.mult))
                then(nc.vector.tensor_tensor(ln_a[:, :], ln_a[:, :], ln_ve[:, :], ALU.mult))
                then(nc.vector.tensor_scalar(ln_a[:, :], ln_a[:, :], -0.5, 1.5, ALU.mult, ALU.add))
                nc.vector.tensor_tensor(rstd[:, :], rstd[:, :], ln_a[:, :], ALU.mult).then_inc(rstd_ready, 1)
                dve.wait_ge(rstd_ready, n)

            nc.vector.memset(xnT[:, 0:BLK], 0.0)
            nc.vector.memset(Kx[:, :, :, 0:BLK], 0.0).then_inc(zeros_ready, 1)
            for b in range(B):
                dve.wait_ge(x_in[b], 16)
                for g in range(b * TPB, (b + 1) * TPB):
                    last = nc.vector.bn_stats(stats[:, g, :], x_all[:, g, :])
            last.then_inc(stats1_done, 1)
            dve.wait_ge(stats1_done, 1)
            ln_moments()
            dve.wait_ge(filled, 1)
            dve.wait_ge(bqkv_in, 16)
            nc.vector.tensor_scalar(bv_wide[:, :], ones[:, 0:P], bqkv_sb[:, 2:3], None, ALU.mult).then_inc(
                bv_wide_ready, 1
            )
            dve.wait_ge(filled, 3)
            nc.vector.tensor_reduce(
                head_of[:, :], ident[:, :].rearrange("p (g h d) -> p h g d", g=NG, d=HD), AX.XY, ALU.add
            ).then_inc(head_of_ready, 1)
            dve.wait_ge(head_of_ready, 1)
            nc.vector.tensor_scalar(bk_of[:, :], head_of[:, :], bqkv_sb[:, 1:2], None, ALU.mult).then_inc(bk_of_ready, 1)
            ln_rstd(1)
            nc.vector.scalar_tensor_tensor(
                out=ln_b[:, :], in0=mean[:, :], scalar=-1.0, in1=rstd[:, :], op0=ALU.mult, op1=ALU.mult
            ).then_inc(shift_ready, 1)
            dve.wait_ge(bias_mm, 1)
            nc.vector.tensor_copy(attn_bias[:, 0, :], psO[:, 0, 0:D]).then_inc(bias_ready, 1)
            dve.wait_ge(bias_ready, 1)
            for _ in range(2):
                nc.vector.memset(esum[:, 0:1], 0.0).then_inc(o_free, 1)
                dve.wait_ge(o_free, 1 + _)

            def find_max(b, k):
                s = psS[:, k % 2, :].rearrange("q (h k) -> q h k", k=KEYS)
                dve.wait_ge(s_done, b * TPB + (k + 1))
                nc.vector.tensor_reduce(row_max[:, k % 2, :], s, AX.X, ALU.max).then_inc(max_done, 1)

            def subtract_max(b, k, first=False):
                s = psS[:, k % 2, :].rearrange("q (h k) -> q h k", k=KEYS)
                dve.wait_ge(max_done, b * TPB + (k + 1))
                if k >= 2 or not first:
                    dve.wait_ge(exp_done, b * TPB + (k - 1))
                nc.vector.tensor_tensor(
                    Sd[:, k % 2, :, :], s, row_max[:, k % 2, :].unsqueeze(2).to_broadcast([P, NH, KEYS]), ALU.subtract
                ).then_inc(sub_done, 1)

            def turn_probs(b, k, first=False):
                dve.wait_ge(exp_done, b * TPB + (k + 1))
                if k >= 2 or not first:
                    dve.wait_ge(pv_done, b * TPB + (k - 1))
                nc.vector.transpose(PT[:, k % 2, :], Pr[:, k % 2, :]).then_inc(pt_done, 1)

            def heads_sums(b, k):
                dve.wait_ge(pv_done, b * TPB + (k + 1))
                o = psO[:, k % 2, 0 : NH * VW].rearrange("q (h j v) -> q h j v", j=NJ, v=VW)
                r = rden[:, k % 2, :].rearrange("q (h j) -> q h j", j=NJ)
                nc.vector.reciprocal(r, o[:, :, :, HD]).then_inc(rden_done, 1)

            def divide_heads(b, k):
                o = psO[:, k % 2, 0 : NH * VW].rearrange("q (h j v) -> q h j v", j=NJ, v=VW)
                r = rden[:, k % 2, :].rearrange("q (h j) -> q h j", j=NJ)
                dve.wait_ge(rden_done, b * TPB + (k + 1))
                nc.vector.tensor_tensor(
                    On[:, k % 2, :].rearrange("q (j h d) -> q h j d", j=NJ, d=HD), o[:, :, :, 0:HD],
                    r.unsqueeze(3).to_broadcast([P, NH // NJ, NJ, HD]), ALU.mult,
                ).then_inc(on_done, 1)

            def turn_heads(b, k):
                dve.wait_ge(on_done, b * TPB + (k + 1))
                nc.vector.transpose(OT[:, k % 2, :], On[:, k % 2, :]).then_inc(ot_done, 1)

            def residual(b, k):
                dve.wait_ge(op_done, b * TPB + (k + 1))
                if k == 0:
                    dve.wait_ge(xb_done, b + 1)
                xk = x_all[:, bass.ds(b * TPB + k, 1), :]
                nc.vector.tensor_tensor(
                    xk, xk, psO[:, k % 2, OPC : OPC + D].unsqueeze(1), ALU.add
                ).then_inc(o_free, 1)

            def moments(b, k):
                at = bass.ds(b * TPB + k, 1)
                dve.wait_ge(o_free, b * TPB + (2 + k + 1))
                nc.vector.bn_stats(
                    stats[:, at, :].rearrange("p a s -> p (a s)"), x_all[:, at, :].rearrange("p a d -> p (a d)")
                ).then_inc(st2_done, 1)

            def tile(b, k, then_b, then_k, before_b, before_k, first=False, last=False):
                if not last:
                    find_max(then_b, then_k)
                turn_probs(b, k, first=first)
                if not last:
                    subtract_max(then_b, then_k, first=first)
                if k > 0 or not first:
                    residual(before_b, before_k)
                heads_sums(b, k)
                if k > 0 or not first:
                    moments(before_b, before_k)
                divide_heads(b, k)
                turn_heads(b, k)

            def batch(b, first=False, last=False):
                tile(b, 0, b, 1, b - 1, TPB - 1, first=first)
                for k in range(1, TPB - 1):
                    tile(b, k, b, k + 1, b, k - 1, first=first)
                tile(b, TPB - 1, b + 1, 0, b, TPB - 2, first=first, last=last)

            find_max(0, 0)
            subtract_max(0, 0, first=True)
            batch(0, first=True)
            with dve.Fori(1, B - 1) as b:
                batch(b)
            batch(B - 1, last=True)
            residual(B - 1, TPB - 1)
            moments(B - 1, TPB - 1)

            dve.wait_ge(st2_done, NT)
            ln_moments()
            ln_rstd(2)
            dve.wait_ge(consts_ready, 2)

            def normalise_rows(b):
                for g in range(b * TPB, (b + 1) * TPB):
                    last = nc.vector.tensor_scalar(
                        rows[:, g, 0, 0:D], x_all[:, g, :], mean[:, g : g + 1], rstd[:, g : g + 1],
                        ALU.subtract, ALU.mult,
                    )
                last.then_inc(rows_ready, 1)

            def shared_hidden(b, c, first=False):
                dve.wait_ge(u_done, b * NC + (c + 1))
                dve.wait_ge(silu_done, b * NC + (c + 1))
                if not first:
                    dve.wait_ge(down_done, b)
                nc.vector.tensor_tensor(hT[:, c, :], psS[:, c % 2, 0:512], sg[:, c % 2, :], ALU.mult).then_inc(h_done, 1)

            def shared_residual(b):
                dve.wait_ge(down_done, b + 1)
                xb = x_all[:, bass.ds(b * TPB, TPB), :]
                nc.vector.tensor_tensor(
                    xb, xb, psO[:, 1, :].rearrange("p (k d) -> p k d", d=D), ALU.add
                ).then_inc(base_done, 1)

            def wide(a):
                return a.unsqueeze(2).to_broadcast([P, NT, E])

            def choose():
                logits = psO[:, 0, 0 : NT * E].rearrange("p (g e) -> p g e", e=E)
                dve.wait_ge(logits_done, NT)
                then(nc.vector.tensor_reduce(top[:, :], logits, AX.X, ALU.max))
                nc.vector.tensor_tensor(logit_d[:, :, :], logits, wide(top[:, :]), ALU.subtract).then_inc(logit_d_ready, 1)
                dve.wait_ge(logit_d_ready, 1)
                then(nc.vector.scalar_tensor_tensor(
                    out=chosen[:, :, :], in0=logit_d[:, :, :], scalar=0.0,
                    in1=rank_of[:, :].unsqueeze(1).to_broadcast([P, NT, E]), op0=ALU.is_ge, op1=ALU.mult,
                ))
                then(nc.vector.tensor_reduce(best[:, :], chosen[:, :, :], AX.X, ALU.max))
                then(nc.vector.tensor_tensor(chosen[:, :, :], chosen[:, :, :], wide(best[:, :]), ALU.is_equal))
                nc.vector.tensor_copy(chosen_h[:, :, :].rearrange("p e g -> p g e"), chosen[:, :, :]).then_inc(chosen_ready, 1)

            def gates():
                then(nc.vector.tensor_scalar(has_expert[:, :], chosen[:, :, NE], -ALPHA, ALPHA, ALU.mult, ALU.add))
                dve.wait_ge(logit_e_ready, 1)
                then(nc.vector.tensor_reduce(esum[:, :], logit_e[:, :, :], AX.X, ALU.add))
                then(nc.vector.reciprocal(esum[:, :], esum[:, :]))
                nc.vector.tensor_tensor(rows[:, :, 0, GATE], esum[:, :], has_expert[:, :], ALU.mult).then_inc(gates_ready, 1)

            flat = "p e g -> p (e g)"

            def count_choices():
                in_tile = psB[:, 0 : E * NT]
                dve.wait_ge(counted, 1)
                then(nc.vector.tensor_tensor_scan(
                    seen[:, :, :].rearrange(flat), ones[:, :], in_tile, 0.0, ALU.mult, ALU.add
                ))
                then(nc.vector.tensor_tensor(
                    pos3[:, :, :].rearrange(flat), seen[:, :, :].rearrange(flat), in_tile, ALU.subtract
                ))
                then(nc.vector.tensor_tensor(count[:, :], seen[:, :, NT - 1], pos3[:, :, 0], ALU.subtract))
                then(nc.vector.tensor_tensor(
                    full[:, :, :], count[:, :].unsqueeze(2).to_broadcast([P, E, NT]),
                    row_no[:, :].unsqueeze(1).to_broadcast([P, E, NT]), ALU.is_gt,
                ))
                then(nc.vector.tensor_reduce(tiles_of[:, :], full[:, :, :], AX.X, ALU.add))

            def place_choices():
                within = psA[:, 0 : E * NT].rearrange("p (e g) -> p e g", e=E)
                then(nc.vector.tensor_tensor_scan(tiles_end[:, :], ones[:, 0:E], tiles_of[:, :], 0.0, ALU.mult, ALU.add))
                then(nc.vector.tensor_tensor(shift[:, :], tiles_end[:, :], tiles_of[:, :], ALU.subtract))
                then(nc.vector.scalar_tensor_tensor(
                    out=shift[:, :], in0=shift[:, :], scalar=float(P), in1=pos3[:, :, 0], op0=ALU.mult, op1=ALU.subtract
                ))
                then(nc.vector.tensor_tensor(pos3[:, :, :], pos3[:, :, :], within, ALU.add))
                then(nc.vector.tensor_tensor(
                    pos3[:, :, :], pos3[:, :, :], shift[:, :].unsqueeze(2).to_broadcast([P, E, NT]), ALU.add
                ))

            def place_tokens():
                then(nc.vector.tensor_tensor(
                    pos3[:, :, :], pos3[:, :, :], chosen[:, :, :].rearrange("p g e -> p e g"), ALU.mult
                ))
                then(nc.vector.tensor_reduce(pos[:, :], pos3[:, :, :].rearrange("p e g -> p g e"), AX.X, ALU.add))
                late = pos[:, (B - LATE) * TPB :]
                then(nc.vector.tensor_scalar(half_pos[:, 0, :], late, 2.0, None, ALU.mult))
                then(nc.vector.tensor_scalar(half_pos[:, 1, :], late, 2.0, 1.0, ALU.mult, ALU.add))
                then(nc.vector.tensor_copy(half_pos_u[:, :, :], half_pos[:, :, :]))
                nc.vector.tensor_copy(pos_u[:, :], pos[:, :]).then_inc(pos_ready, 1)

            def experts_of_tiles():
                then(nc.vector.tensor_tensor(
                    past[:, :, :], tile_no[:, :].unsqueeze(2).to_broadcast([P, MT, NE]),
                    tiles_end[:, 0:NE].unsqueeze(1).to_broadcast([P, MT, NE]), ALU.is_ge,
                ))
                then(nc.vector.tensor_reduce(tile_e[:, :], past[:, :, :], AX.X, ALU.add))
                then(nc.vector.tensor_scalar(
                    tile_e[:, :], tile_e[:, :], float(NE - 1), float(HID), ALU.min, ALU.mult
                ))
                nc.vector.tensor_copy(tile_at[:, :], tile_e[:, :]).then_inc(tile_at_ready, 1)

            normalise_rows(0)
            normalise_rows(1)
            for c in range(NC - 1):
                normalise_rows(2 * c + 2)
                shared_hidden(0, c, first=True)
                normalise_rows(2 * c + 3)
            shared_hidden(0, NC - 1, first=True)
            shared_hidden(1, 0)
            choose()
            shared_residual(0)
            shared_hidden(1, 1)
            shared_hidden(1, 2)
            gates()
            shared_hidden(1, 3)
            count_choices()
            shared_hidden(2, 0)
            place_choices()
            shared_residual(1)
            shared_hidden(2, 1)
            place_tokens()
            shared_hidden(2, 2)
            experts_of_tiles()
            shared_hidden(2, 3)
            with dve.Fori(3, B) as b:
                shared_hidden(b, 0)
                shared_residual(b - 1)
                for c in range(1, NC):
                    shared_hidden(b, c)
            shared_residual(B - 1)

            def expert_step(s, r, ug=True, down=True):
                if down:
                    q = (r - 2) % RING
                    dve.wait_ge(ey_done, s - 1)
                    dve.wait_ge(base_in[q], loads(s - 2, r - 2))
                    nc.vector.tensor_tensor(y[:, q, :], psB[:, 0:D], base[:, q, :], ALU.add).then_inc(y_ready, 1)
                if ug:
                    q = r % RING
                    dve.wait_ge(xs_in[q], loads(s, r))
                    if r >= RING:
                        dve.wait_ge(written[q], loads(s, r) - 16)
                    nc.vector.tensor_copy(tok_u[:, q : q + 1], xs[:, q, TOKEN : TOKEN + 1]).then_inc(tok_ready, 1)
                    dve.wait_ge(eu_done, s + 1)
                    dve.wait_ge(esilu_done, s + 1)
                    if r >= 2:
                        dve.wait_ge(ehT_done, s - 1)
                    nc.vector.scalar_tensor_tensor(
                        out=hs[:, r % 2, :], in0=psS[:, r % 2, 0:512], scalar=xs[:, q, GATE : GATE + 1],
                        in1=sg[:, r % 2, :], op0=ALU.mult, op1=ALU.mult,
                    ).then_inc(eh_done, 1)

            for s in range(RING + 2):
                expert_step(s, s, down=s >= 2)
            with dve.Fori(RING + 2, MT - RING, RING) as s:
                for r in range(RING):
                    expert_step(s + r, RING + 2 + r)
            expert_step(MT - 1, MT - 1)
            expert_step(MT, MT, ug=False)
            expert_step(MT + 1, MT + 1, ug=False)

        @block.tensor
        def _(pe):
            mm = nc.tensor.matmul
            pe.wait_ge(bv_wide_ready, 1)
            pe.wait_ge(wout_in, 16)
            pe.wait_ge(bout_in, 16)
            mm(psO[:, 0, 0:D], bv_wide[:, :], wout_sb[:, :], start=True, stop=False)
            mm(psO[:, 0, 0:D], ones[0:1, 0:P], bout_sb[0:1, :], start=False, stop=True).then_inc(bias_mm, 1)

            def turn_x(n):
                pe.wait_ge(norm_done, n)
                for k in range(TPB):
                    last = nc.tensor.transpose(psA[:, k * P : (k + 1) * P], xn[:, k, :], ident[:, :])
                last.then_inc(xt_done, 1)

            def queries_keys(n, first=False):
                pe.wait_ge(xnT_ready, n)
                mm(psA[:, :], wqkv_sb[:, 0:D], xnT[:, BLK:], start=True, stop=True).then_inc(qk_done, 1)
                if not first:
                    pe.wait_ge(v_ready, 2 * NJ * (n - 1))
                mm(psB[:, :], wqkv_sb[:, D : 2 * D], xnT[:, BLK:], start=True, stop=True).then_inc(qk_done, 1)

            def values(half, bank):
                for t in range(2):
                    k = 2 * half + t
                    for c in range(2):
                        at = k * P + c * BLK
                        col = (2 * t + c) * D
                        last = mm(bank[:, col : col + D], xnT[:, at : at + P], wqkv_sb[:, 2 * D :], start=True, stop=True)
                last.then_inc(v_done, 1)

            def scores(b, odd, k, first=False):
                if k == 0:
                    pe.wait_ge(q_ready, b + 1)
                    pe.wait_ge(k_ready, b + 1)
                if k >= 2 or not first:
                    pe.wait_ge(sub_done, b * TPB + (k - 1))
                variant = 0 if k == 0 else 1
                for half in range(2):
                    s = psS[:, k % 2, 512 * half : 512 * (half + 1)]
                    mm(s, ident_h[:, :], mask_h[:, variant, :, :], start=True, stop=False, skip_group_check=True)
                    for gg in range(HPB // HPG):
                        g = half * (HPB // HPG) + gg
                        for j in range(NJ):
                            at = k * P + j * BLK
                            last = mm(
                                s[j * BLK : (j + 1) * BLK, gg * HPG * KEYS : (gg + 1) * HPG * KEYS],
                                Qx[:, odd, g, at : at + BLK], Kx[:, odd, :, at : at + KEYS],
                                start=False, stop=True, skip_group_check=True,
                            )
                last.then_inc(s_done, 1)

            def weigh_values(b, k):
                pe.wait_ge(pt_done, b * TPB + (k + 1))
                pe.wait_ge(o_free, b * TPB + (k + 1))
                if k % 2 == 0:
                    pe.wait_ge(v_ready, 2 * NJ * b + (k // 2 + 1) * NJ)
                for hh in range(NH // NJ):
                    for c in range(2):
                        for g in range(NJ):
                            h = g * (NH // NJ) + hh
                            last = mm(
                                psO[g * BLK : (g + 1) * BLK, k % 2, hh * NJ * VW : (hh + 1) * NJ * VW],
                                PT[:, k % 2, (2 * h + c) * BLK : (2 * h + c + 1) * BLK],
                                VD[:, k, c, h, :, :].rearrange("k j v -> k (j v)"),
                                start=(c == 0), stop=(c == 1),
                            )
                last.then_inc(pv_done, 1)

            def project(b, k):
                pe.wait_ge(ot_done, b * TPB + (k + 1))
                mm(psO[:, k % 2, OPC : OPC + D], OT[:, k % 2, :], wout_sb[:, :], start=True, stop=True).then_inc(
                    op_done, 1
                )

            pe.wait_ge(filled, 4)
            pe.wait_ge(zeros_ready, 1)
            turn_x(1)
            pe.wait_ge(wqkv_in, 16)
            queries_keys(1)
            pe.wait_ge(q_ready, 1)
            values(0, psA)
            pe.wait_ge(k_ready, 1)
            values(1, psB)
            pe.wait_ge(consts_ready, 1)
            scores(0, 0, 0, first=True)
            scores(0, 0, 1, first=True)
            pe.wait_ge(v_ready, NJ)
            turn_x(2)
            scores(0, 0, 2)

            def batch(b, odd, qkv=True, xt=True):
                if qkv:
                    queries_keys(b + 2)
                weigh_values(b, 0)
                scores(b, odd, 3)
                project(b, 0)
                weigh_values(b, 1)
                if qkv:
                    scores(b + 1, 1 - odd, 0)
                project(b, 1)
                if qkv:
                    values(0, psA)
                    values(1, psB)
                weigh_values(b, 2)
                if qkv:
                    scores(b + 1, 1 - odd, 1)
                project(b, 2)
                if xt:
                    pe.wait_ge(v_ready, 2 * NJ * b + (2 * NJ + NJ))
                    turn_x(b + 3)
                weigh_values(b, 3)
                if qkv:
                    scores(b + 1, 1 - odd, 2)
                project(b, 3)

            batch(0, 0)
            with pe.Fori(1, B - 3, 2) as b:
                batch(b, 1)
                batch(b + 1, 0)
            batch(B - 3, 1)
            batch(B - 2, 0, xt=False)
            batch(B - 1, 1, qkv=False, xt=False)

            def turn_rows(b):
                pe.wait_ge(rows_ready, b + 1)
                if b >= 2:
                    pe.wait_ge(xn2T_ready, b - 1)
                for k in range(TPB):
                    bank = (psA, psB)[b % 2]
                    last = nc.tensor.transpose(bank[:, k * P : (k + 1) * P], rows[:, b * TPB + k, 0, 0:D], ident[:, :])
                last.then_inc(rows_turned, 1)

            def route(b):
                pe.wait_ge(xn2T_ready, b + 1)
                for g in range(b * TPB, (b + 1) * TPB):
                    mm(
                        psO[:, 0, g * E : (g + 1) * E], xn2T[:, g * P : (g + 1) * P], wr_sb[:, :], start=True, stop=True
                    ).then_inc(logits_done, 1)

            def rank_tokens():
                pe.wait_ge(chosen_ready, 1)
                ch = chosen_h[:, :, :].rearrange("p e g -> p (e g)")
                mm(psA[:, 0 : E * NT], before_h[:, :], ch, start=True, stop=True)
                mm(psB[:, 0 : E * NT], ones_h[:, :], ch, start=True, stop=True).then_inc(counted, 1)

            def shared_up(b, c, first=False):
                if c >= 2 or not first:
                    pe.wait_ge(h_done, b * NC + (c - 1))
                xt = xn2T[:, bass.ds(b * T, T)]
                w = slice(c * P, (c + 1) * P)
                mm(psS[:, c % 2, 512:], gate_sb[:, SHARED, w], xt, start=True, stop=True).then_inc(g_done, 1)
                mm(psS[:, c % 2, 0:512], up_sb[:, SHARED, w], xt, start=True, stop=True).then_inc(u_done, 1)

            def shared_down(b, first=False):
                pe.wait_ge(h_done, b * NC + NC)
                if not first:
                    pe.wait_ge(base_done, b)
                for k in range(TPB):
                    for c in range(NC):
                        last = mm(
                            psO[:, 1, k * D : (k + 1) * D], hT[:, c, k * P : (k + 1) * P],
                            down_sb[:, SHARED, c * D : (c + 1) * D], start=(c == 0), stop=(c == NC - 1),
                        )
                last.then_inc(down_done, 1)

            turn_rows(0)
            turn_rows(1)
            pe.wait_ge(wr_in, 16)
            route(0)
            for n in range(3):
                pe.wait_ge(shared_in[n], 16)
            for c in range(NC - 1):
                shared_up(0, c, first=True)
                turn_rows(2 * c + 2)
                route(2 * c + 1)
                turn_rows(2 * c + 3)
                route(2 * c + 2)
            shared_up(0, NC - 1)
            route(B - 1)
            shared_up(1, 0)
            shared_down(0, first=True)
            for c in range(1, NC):
                shared_up(1, c)
            rank_tokens()
            with pe.Fori(2, B) as b:
                shared_up(b, 0)
                shared_down(b - 1)
                for c in range(1, NC):
                    shared_up(b, c)
            shared_down(B - 1)

            up_flat = up_sb[:, :, :].rearrange("p e h -> p (e h)")
            gate_flat = gate_sb[:, :, :].rearrange("p e h -> p (e h)")
            down_flat = down_sb[:, :, :].rearrange("p e h -> p (e h)")

            def expert_turn_rows(i, r):
                pe.wait_ge(xs_in[r % RING], loads(i, r))
                if r >= 1:
                    pe.wait_ge(xsT_ready, i)
                nc.tensor.transpose(psA[:, 0:P], xs[:, r % RING, 0:D], ident[:, :]).then_inc(xsT_done, 1)

            def weights_of(i):
                return pe.value_load(tile_at[0:1, bass.ds(i, 1)], min_val=0, max_val=(NE - 1) * HID)

            def expert_step(s, r, ug=True, ht=True, xt=True, down=True):
                if ug:
                    w = bass.ds(weights_of(s), HID)
                if down:
                    at = weights_of(s - 2)
                    pe.wait_ge(ehT_ready, s - 1)
                    if r >= 3:
                        pe.wait_ge(y_ready, s - 2)
                    for c in range(NC):
                        last = mm(
                            psB[:, 0:D], hsT[:, r % 2, c * P : (c + 1) * P], down_flat[:, bass.ds(at + c * D, D)],
                            start=(c == 0), stop=(c == NC - 1),
                        )
                    last.then_inc(ey_done, 1)
                if xt:
                    expert_turn_rows(s + 1, r + 1)
                if ug:
                    pe.wait_ge(xsT_ready, s + 1)
                    if r >= 2:
                        pe.wait_ge(eh_done, s - 1)
                    mm(psS[:, r % 2, 512:], xsT[:, r % 2, :], gate_flat[:, w], start=True, stop=True).then_inc(eg_done, 1)
                if ht:
                    pe.wait_ge(eh_done, s)
                    for c in range(NC):
                        hidden = slice(c * P, (c + 1) * P)
                        last = nc.tensor.transpose(psO[:, (r + 1) % 2, hidden], hs[:, (r + 1) % 2, hidden], ident[:, :])
                    last.then_inc(ehT_done, 1)
                if ug:
                    mm(psS[:, r % 2, 0:512], xsT[:, r % 2, :], up_flat[:, w], start=True, stop=True).then_inc(eu_done, 1)

            for n in range(3):
                pe.wait_ge(experts_in[n], 16)
            pe.wait_ge(tile_at_ready, 1)
            expert_turn_rows(0, 0)
            for s in range(RING + 2):
                expert_step(s, s, ht=s >= 1, down=s >= 2)
            with pe.Fori(RING + 2, MT - RING, RING) as s:
                for r in range(RING):
                    expert_step(s + r, RING + 2 + r)
            expert_step(MT - 1, MT - 1, xt=False)
            expert_step(MT, MT, ug=False, xt=False)
            expert_step(MT + 1, MT + 1, ug=False, ht=False, xt=False)


_INS = [
    "L0_attn_x", "L0_attn_W_qkv", "L0_attn_b_qkv", "L0_attn_W_out", "L0_attn_b_out", "L0_ffn_w_router",
    "L0_ffn_w_up", "L0_ffn_w_gate", "L0_ffn_w_down", "L0_ffn_ws_up", "L0_ffn_ws_gate", "L0_ffn_ws_down",
]


def kernel(**inputs):
    import concourse.bacc as bacc
    import numpy as np
    from concourse.bass_utils import run_bass_kernel_spmd

    nc = bacc.Bacc("TRN2", target_bir_lowering=False, num_devices=1)
    arrays, args = {}, []
    for name in _INS:
        a = np.ascontiguousarray(inputs[name])
        arrays[f"in_{name}"] = a
        args.append(nc.dram_tensor(f"in_{name}", a.shape, mybir.dt.from_np(a.dtype), kind="ExternalInput").ap())
    x = arrays["in_L0_attn_x"]
    args.append(nc.dram_tensor("out", x.shape, mybir.dt.from_np(x.dtype), kind="ExternalOutput").ap())
    windowed_attention_top1_moe_kernel(nc, *args)
    return run_bass_kernel_spmd(nc, [arrays], core_ids=[0]).results[0]["out"]
```

```python
import math
from contextlib import ExitStack

import concourse.bass as bass
from concourse import mybir


def windowed_attention_top1_moe_kernel(
    nc, x, w_qkv, b_qkv, w_out, b_out, w_router, w_up, w_gate, w_down, ws_up, ws_gate, ws_down, out
):
    f32, f32r, bf16 = mybir.dt.float32, mybir.dt.float32r, mybir.dt.bfloat16
    i32, u32 = mybir.dt.int32, mybir.dt.uint32
    ALU = mybir.AluOpType
    ACT = mybir.ActivationFunctionType
    AX = mybir.AxisListType

    B, T, D = x.shape
    P = 128
    NH, HD, WIN = 16, 8, 32
    BLK = 32
    NJ = P // BLK
    KEYS = 2 * BLK
    HPB = 512 // KEYS
    HPG = BLK // HD
    NG = NH // HPG
    TPB = T // P
    NT = B * TPB
    E = w_router.shape[1]
    NE = E - 1
    HID = w_up.shape[2]
    NC = HID // P
    SHARED = NE
    MT = (NT * P - E) // P + E
    GATE, TOKEN = D, D + 1
    ROW = D + 4
    LATE = 2
    WARM = 96
    WARM_LAST = (12, 12, 20, 20, 36)
    RING = 4
    NOBODY = 2.0 * NT * P
    ALPHA, EPS = 2.0, 1e-5
    MASKED = -1e30
    SCALE = 1.0 / math.sqrt(HD)
    VW = HD + 1

    ctx = ExitStack()
    with ctx:

        place = {}

        def sb(name, shape, dt=f32):
            place[name] = nc.sbuf_base
            return ctx.enter_context(nc.sbuf_tensor(name, shape, dt))

        def sb_over(old, name, shape, dt=f32):
            return nc.alloc_sbuf_tensor_at(name, shape, dt, offset=place[old])

        def sem(name):
            return ctx.enter_context(nc.semaphore(name))

        wqkv_sb = sb("wqkv_sb", [P, 3 * D])
        bqkv_sb = sb("bqkv_sb", [P, 3])
        wout_sb = sb("wout_sb", [P, D])
        bout_sb = sb("bout_sb", [1, D])
        wr_sb = sb("wr_sb", [P, E])
        up_sb = sb("up_sb", [P, E, HID])
        gate_sb = sb("gate_sb", [P, E, HID])
        down_sb = sb("down_sb", [P, E, NC * D])
        ones = sb("ones", [P, NT * E])
        ident = sb("ident", [P, P])
        ident_h = sb("ident_h", [P, P], bf16)
        ones_h = sb("ones_h", [P, P], bf16)
        before_h = sb("before_h", [P, P], bf16)
        block_mask = sb("block_mask", [P, KEYS], bf16)
        mask_h = sb("mask_h", [P, 2, HPB, KEYS], bf16)
        head_of = sb("head_of", [P, HPG])
        bk_of = sb("bk_of", [P, HPG])
        bv_wide = sb("bv_wide", [P, P])
        attn_bias = sb("attn_bias", [P, 1, D])
        rows = sb("rows", [P, NT, 2, ROW])
        x_all = rows[:, :, 1, 0:D]
        stats = sb("stats", [P, NT, 6])
        ln_a = sb("ln_a", [P, NT])
        ln_b = sb("ln_b", [P, NT])
        ln_ve = sb("ln_ve", [P, NT])
        ln_sd = sb("ln_sd", [P, NT])
        mean = sb("mean", [P, NT])
        rstd = sb("rstd", [P, NT])
        xn = sb("xn", [P, TPB, D])
        xnT = sb("xnT", [P, T])
        Qx = sb("Qx", [P, 2, NG, T])
        Kx = sb("Kx", [P, 2, HPG, BLK + T])
        VD = sb("VD", [P, TPB, 2, NH, NJ, VW])
        row_max = sb("row_max", [P, 2, NH])
        Sd = sb("Sd", [P, 2, NH, KEYS])
        Pr = sb("Pr", [P, 2, NH * KEYS])
        PT = sb("PT", [P, 2, NH * KEYS])
        rden = sb("rden", [P, 2, NH])
        On = sb("On", [P, 2, D])
        OT = sb("OT", [P, 2, D])

        xn2T = sb("xn2T", [P, NT * P])
        top = sb("top", [P, NT])
        chosen = sb("chosen", [P, NT, E])
        best = sb("best", [P, NT])
        chosen_h = sb("chosen_h", [P, E, NT], bf16)
        logit_d = sb("logit_d", [P, NT, E])
        logit_e = sb("logit_e", [P, NT, E])
        esum = sb("esum", [P, NT])
        has_expert = sb("has_expert", [P, NT])
        rank_of = sb("rank_of", [P, E])
        tile_no = sb("tile_no", [P, MT])
        row_no = sb("row_no", [P, NT])
        seen = sb("seen", [P, E, NT])
        count = sb("count", [P, E])
        full = sb("full", [P, E, NT])
        tiles_of = sb("tiles_of", [P, E])
        tiles_end = sb("tiles_end", [P, E])
        shift = sb("shift", [P, E])
        pos3 = sb("pos3", [P, E, NT])
        pos = sb("pos", [P, NT])
        pos_u = sb("pos_u", [P, NT], u32)
        half_pos = sb("half_pos", [P, 2, LATE * TPB])
        half_pos_u = sb("half_pos_u", [P, 2, LATE * TPB], u32)
        past = sb("past", [P, MT, NE])
        tile_e = sb("tile_e", [P, MT])
        tile_at = sb("tile_at", [P, MT], i32)
        pad_row = sb("pad_row", [P, 1, 2 * ROW])
        sg = PT[:, 0, :].rearrange("p (a h) -> p a h", a=2)
        hT = Sd[:, :, :, :].rearrange("p a h k -> p (a h k)").rearrange("p (c t) -> p c t", c=NC)
        gate_hi = sb_over("Qx", "gate_hi", [P, E * HID], f32r)
        up_hi = sb_over("Kx", "up_hi", [P, E * HID], f32r)
        xn2T_hi = sb_over("VD", "xn2T_hi", [P, NT * P], f32r)
        gate_lo = sb_over("gate_sb", "gate_lo", [P, E * HID], f32r)
        up_lo = sb_over("up_sb", "up_lo", [P, E * HID], f32r)
        xn2T_lo = sb_over("xn2T", "xn2T_lo", [P, NT * P], f32r)
        xs = sb("xs", [P, RING, ROW])
        base = sb("base", [P, RING, D])
        tok_u = sb("tok_u", [P, RING], u32)
        xsT = sb("xsT", [P, 2, 2, P], f32r)
        hs = Pr[:, 0, :].rearrange("p (a h) -> p a h", a=2)
        hsT = Pr[:, 1, :].rearrange("p (a h) -> p a h", a=2)
        y = sb("y", [P, RING, D])
        sorted_rows = nc.dram_tensor("sorted_rows", [MT * P, 2 * ROW], f32, kind="Internal").ap()
        sorted_halves = sorted_rows.rearrange("t (a r) -> (t a) r", a=2)

        psS = ctx.enter_context(nc.psum_tensor("psS", [P, 2, 1024], f32))
        psO = ctx.enter_context(nc.psum_tensor("psO", [P, 2, 512], f32))
        psA = ctx.enter_context(nc.psum_tensor("psA", [P, 512], f32))
        psB = ctx.enter_context(nc.psum_tensor("psB", [P, 512], f32))
        OPC = 256

        x_in = [sem(f"x_in{b}") for b in range(B)]
        wqkv_in, bqkv_in = sem("wqkv_in"), sem("bqkv_in")
        wout_in, bout_in = sem("wout_in"), sem("bout_in")
        filled, consts_ready, bv_wide_ready = sem("filled"), sem("consts_ready"), sem("bv_wide_ready")
        bias_mm, bias_ready = sem("bias_mm"), sem("bias_ready")
        zeros_ready, head_of_ready, bk_of_ready = sem("zeros_ready"), sem("head_of_ready"), sem("bk_of_ready")
        ln_step, ln_sd_ready, stats1_done = sem("ln_step"), sem("ln_sd_ready"), sem("stats1_done")
        shift_ready = sem("shift_ready")
        ln_ve_ready = sem("ln_ve_ready")
        norm_done, xt_done, xnT_ready = sem("norm_done"), sem("xt_done"), sem("xnT_ready")
        qk_done, q_ready, k_ready = sem("qk_done"), sem("q_ready"), sem("k_ready")
        v_done, v_ready = sem("v_done"), sem("v_ready")
        s_done, max_done, sub_done = sem("s_done"), sem("max_done"), sem("sub_done")
        exp_done, pt_done, pv_done = sem("exp_done"), sem("pt_done"), sem("pv_done")
        rden_done, on_done, ot_done = sem("rden_done"), sem("on_done"), sem("ot_done")
        op_done = sem("op_done")
        o_free = sem("o_free")
        xb_done, st2_done = sem("xb_done"), sem("st2_done")
        wr_in, shared_in, experts_in = sem("wr_in"), [sem(f"shared_in{n}") for n in range(3)], [
            sem(f"experts_in{n}") for n in range(3)
        ]
        pads_written, pad_ready, rows_turned = sem("pads_written"), sem("pad_ready"), sem("rows_turned")
        rows_ready, xn2T_ready, logits_done = sem("rows_ready"), sem("xn2T_ready"), sem("logits_done")
        logit_d_ready, logit_e_ready = sem("logit_d_ready"), sem("logit_e_ready")
        chosen_ready, counted, gates_ready, pos_ready = (
            sem("chosen_ready"), sem("counted"), sem("gates_ready"), sem("pos_ready"),
        )
        tile_at_ready = sem("tile_at_ready")
        shared_split, experts_split = sem("shared_split"), sem("experts_split")
        xn2T_hi_ready, xn2T_lo_ready, xsT_lo_ready = sem("xn2T_hi_ready"), sem("xn2T_lo_ready"), sem("xsT_lo_ready")
        x_scattered, base_scattered = sem("x_scattered"), sem("base_scattered")
        g_done, u_done, silu_done, h_done, down_done, base_done = (
            sem("g_done"), sem("u_done"), sem("silu_done"), sem("h_done"), sem("down_done"), sem("base_done"),
        )
        xs_in = [sem(f"xs_in{r}") for r in range(RING)]
        base_in = [sem(f"base_in{r}") for r in range(RING)]
        written = [sem(f"written{r}") for r in range(RING)]
        xsT_done, xsT_ready = sem("xsT_done"), sem("xsT_ready")
        eg_done, eu_done, esilu_done = sem("eg_done"), sem("eu_done"), sem("esilu_done")
        eh_half, eh_done = sem("eh_half"), sem("eh_done")
        ehT_done, ehT_ready = sem("ehT_done"), sem("ehT_ready")
        ey_done, y_ready = sem("ey_done"), sem("y_ready")

        def loads(i, r):
            q = r % RING
            return 16 * (i // RING + 1) if isinstance(i, int) else i * (16 // RING) + (16 - (16 // RING) * q)

        x_rows = x.rearrange("b (k p) d -> p (b k) d", p=P)

        block = ctx.enter_context(nc.Block())

        after = {}

        @block.sync
        def _(sp):
            for b in range(B):
                sp.dma_start(x_all[:, b * TPB : (b + 1) * TPB, :], x_rows[:, b * TPB : (b + 1) * TPB, :]).then_inc(
                    x_in[b], 16
                )

            sp.dma_start(wr_sb[:, :], w_router).then_inc(wr_in, 16)
            sp.dma_start(up_sb[:, SHARED, :], ws_up).then_inc(shared_in[0], 16)
            sp.dma_start(gate_sb[:, SHARED, :], ws_gate).then_inc(shared_in[1], 16)
            sp.dma_start(
                down_sb[:, SHARED, :].rearrange("p (c d) -> p c d", d=D), ws_down.rearrange("(c p) d -> p c d", p=P)
            ).then_inc(shared_in[2], 16)
            sp.dma_start(up_sb[:, 0:NE, :], w_up.rearrange("e p h -> p e h")).then_inc(experts_in[0], 16)
            sp.dma_start(gate_sb[:, 0:NE, :], w_gate.rearrange("e p h -> p e h")).then_inc(experts_in[1], 16)
            sp.dma_start(
                down_sb[:, 0:NE, :].rearrange("p e (c d) -> p (e c) d", d=D),
                w_down.rearrange("e (c p) d -> p (e c) d", p=P),
            ).then_inc(experts_in[2], 16)
            sp.wait_ge(pad_ready, 1)
            sp.dma_start(
                sorted_rows.rearrange("(i p) r -> p i r", p=P), pad_row[:, :, :].to_broadcast([P, MT, 2 * ROW])
            ).then_inc(pads_written, 16)

            def load(i, r, wait=True):
                if wait:
                    sp.wait_ge(eh_done, i - (RING - 1))
                sp.dma_start(xs[:, r, :], sorted_rows[bass.ds(i * P, P), 0:ROW]).then_inc(xs_in[r], 16)

            def load_base(i, r, wait=True):
                if wait:
                    sp.wait_ge(y_ready, i - (RING - 1))
                sp.dma_start(base[:, r, :], sorted_rows[bass.ds(i * P, P), ROW : ROW + D]).then_inc(base_in[r], 16)

            sp.wait_ge(x_scattered, 16 * NT)
            for i in range(RING):
                load(i, i, wait=False)
            sp.wait_ge(base_scattered, 16 * LATE * TPB)
            for i in range(RING):
                load_base(i, i, wait=False)
            with sp.Fori(RING, MT - MT % RING - RING + 1, RING) as i:
                for r in range(RING):
                    load(i + r, r)
                    load_base(i + r, r)
            for i in range(MT - MT % RING, MT):
                load(i, i % RING)
                load_base(i, i % RING)

        @block.gpsimd
        def _(pool):
            made = [0]

            def make(ins):
                made[0] += 1
                ins.then_inc(filled, 1)
                pool.wait_ge(filled, made[0])

            make(pool.memset(ones_h[:, :], 1.0))
            after["ones_h"] = made[0]
            make(pool.memset(ones[:, :], 1.0))
            after["ones"] = made[0]
            make(pool.memset(ident[:, :], 0.0))
            make(pool.affine_select(
                out=ident[:, :], in_=ident[:, :], compare_op=ALU.not_equal, fill=1.0,
                base=0, pattern=[[-1, P]], channel_multiplier=1,
            ))
            after["ident"] = made[0]
            make(pool.memset(block_mask[:, :], 0.0))
            for j in range(NJ):
                m = block_mask[j * BLK : (j + 1) * BLK, :]
                make(pool.affine_select(
                    out=m, in_=m, compare_op=ALU.is_ge, fill=MASKED,
                    base=BLK, pattern=[[-1, KEYS]], channel_multiplier=1,
                ))
                make(pool.affine_select(
                    out=m, in_=m, compare_op=ALU.is_ge, fill=MASKED,
                    base=WIN - BLK - 1, pattern=[[1, KEYS]], channel_multiplier=-1,
                ))
            make(pool.tensor_copy(
                mask_h[:, :, :, :].rearrange("q a h k -> q (a h) k"),
                block_mask[:, :].unsqueeze(1).to_broadcast([P, 2 * HPB, KEYS]),
            ))
            make(pool.memset(mask_h[0:BLK, 0, :, 0:BLK], MASKED))
            make(pool.tensor_copy(ident_h[:, :], ident[:, :]))
            after["masks"] = made[0]
            make(pool.memset(VD[:, :, :, :, :, :], 0.0))
            for j in range(NJ):
                r = slice(j * BLK, (j + 1) * BLK)
                make(pool.memset(VD[r, :, :, :, j, HD].rearrange("k t c h -> k (t c h)"), 1.0))
            after["VD"] = made[0]
            make(pool.memset(Qx[:, 1, :, :], 0.0))
            after["Qx 1"] = made[0]
            make(pool.affine_select(
                out=before_h[:, :], in_=ones_h[:, :], compare_op=ALU.is_gt, fill=0.0,
                base=0, pattern=[[1, P]], channel_multiplier=-1,
            ))
            make(pool.memset(pad_row[:, :, 0:TOKEN], 0.0))
            pool.memset(pad_row[:, :, TOKEN:], NOBODY).then_inc(pad_ready, 1)
            made_up_to = dict(channel_multiplier=0, allow_small_or_imprecise_dtypes=True)
            make(pool.iota(rank_of[:, :], [[-1, E]], base=E, **made_up_to))
            make(pool.iota(tile_no[:, :], [[1, MT]], base=0, **made_up_to))
            make(pool.iota(row_no[:, :], [[P, NT]], base=0, **made_up_to))
            make(pool.memset(rows[:, :, 0, TOKEN + 1 :], 0.0))
            make(pool.memset(rows[:, :, 1, D:], 0.0))
            pool.iota(
                rows[:, :, 0, TOKEN : TOKEN + 1], [[P, NT], [0, 1]], base=0, channel_multiplier=1,
                allow_small_or_imprecise_dtypes=True,
            ).then_inc(consts_ready, 1)

            def add_bias(b):
                pool.wait_ge(norm_done, b + 1)
                xb = x_all[:, bass.ds(b * TPB, TPB), :]
                pool.tensor_tensor(xb, xb, attn_bias[:, :, :].to_broadcast([P, TPB, D]), ALU.add).then_inc(xb_done, 1)

            pool.wait_ge(bias_ready, 1)
            with pool.Fori(0, B) as b:
                add_bias(b)

            def split(hi, whole, lo, columns, done):
                hi, whole, lo = hi[:, columns], whole[:, columns], lo[:, columns]
                make(pool.tensor_copy(hi, whole))
                pool.tensor_tensor(lo, whole, hi.bitcast(f32), ALU.subtract).then_inc(done, 1)

            gate_flat = gate_sb[:, :, :].rearrange("p e h -> p (e h)")
            up_flat = up_sb[:, :, :].rearrange("p e h -> p (e h)")
            pool.wait_ge(s_done, NT)
            for n in range(2):
                pool.wait_ge(shared_in[n], 16)
            split(gate_hi, gate_flat, gate_lo, slice(SHARED * HID, E * HID), shared_split)
            split(up_hi, up_flat, up_lo, slice(SHARED * HID, E * HID), shared_split)
            for n in range(2):
                pool.wait_ge(experts_in[n], 16)
            split(gate_hi, gate_flat, gate_lo, slice(0, NE * HID), experts_split)
            split(up_hi, up_flat, up_lo, slice(0, NE * HID), experts_split)

            def scatter(g):
                pool.indirect_dma_start(
                    out=sorted_rows, out_offset=bass.IndirectOffsetOnAxis(pos_u[:, g : g + 1], 0),
                    in_=rows[:, g, :, :].rearrange("p a r -> p (a r)"), in_offset=None,
                ).then_inc(x_scattered, 16)

            def scatter_half(g, half, done):
                n = g - (B - LATE) * TPB
                pool.indirect_dma_start(
                    out=sorted_halves, out_offset=bass.IndirectOffsetOnAxis(half_pos_u[:, half, n : n + 1], 0),
                    in_=rows[:, g, half, :], in_offset=None,
                ).then_inc(done, 16)

            pool.wait_ge(pads_written, 16)
            pool.wait_ge(gates_ready, 1)
            pool.wait_ge(pos_ready, 1)
            for g in range((B - LATE) * TPB, NT):
                scatter_half(g, 0, x_scattered)
            for g in range(NT):
                if g >= (B - 1) * TPB:
                    pool.wait_ge(base_done, g - (B - 1) * (TPB - 1) + 1)
                elif g % TPB == 0:
                    pool.wait_ge(base_done, g // TPB + 1)
                if g < (B - LATE) * TPB:
                    scatter(g)
                else:
                    scatter_half(g, 1, base_scattered)

            last_token = pool.to_reg(NT * P - 1)
            out_list = out.rearrange("b t d -> (b t) d")

            def write(i, r):
                pool.wait_ge(y_ready, i + 1)
                pool.indirect_dma_start(
                    out=out_list, out_offset=bass.IndirectOffsetOnAxis(tok_u[:, r : r + 1], 0),
                    in_=y[:, r, :], in_offset=None, bounds_check=last_token, oob_is_err=False,
                ).then_inc(written[r], 16)

            for i in range(MT):
                write(i, i % RING)
            for r in range(RING):
                pool.wait_ge(written[r], 16 * ((MT - 1 - r) // RING + 1))

        @block.scalar
        def _(act):
            act.dma_start(wqkv_sb[:, :], w_qkv).then_inc(wqkv_in, 16)
            act.dma_start(bqkv_sb[:, :], b_qkv.rearrange("(t p) -> p t", p=P), allow_slow_non_contiguous=True).then_inc(bqkv_in, 16)
            act.dma_start(wout_sb[:, :], w_out).then_inc(wout_in, 16)
            act.dma_start(bout_sb[:, :], b_out.rearrange("(a n) -> a n", a=1)).then_inc(bout_in, 16)

            def deviations(lo, hi, n):
                act.wait_ge(ln_ve_ready, n)
                nc.scalar.activation(ln_sd[:, lo:hi], ln_ve[:, lo:hi], ACT.Sqrt).then_inc(ln_sd_ready, 1)

            deviations(0, TPB, 1)

            def evict_xnT(n, first=False):
                act.wait_ge(xt_done, n)
                if not first:
                    act.wait_ge(v_done, n - 1)
                nc.scalar.copy(xnT[:, :], psA[:, :]).then_inc(xnT_ready, 1)

            def evict_q(n, odd):
                act.wait_ge(qk_done, 2 * n - 1)
                for g in range(NG):
                    r = slice(g * BLK, (g + 1) * BLK)
                    last = nc.scalar.activation(Qx[r, odd, g, :], psA[r, :], ACT.Identity, bias=bqkv_sb[r, 0:1])
                last.then_inc(q_ready, 1)

            def evict_k(n, odd):
                act.wait_ge(qk_done, 2 * n)
                for h in range(HPG):
                    last = nc.scalar.activation(
                        Kx[:, odd, h, BLK:], psB[:, :], ACT.Identity, bias=bk_of[:, h : h + 1], scale=head_of[:, h : h + 1]
                    )
                last.then_inc(k_ready, 1)

            def evict_v(n, half, bank=psB, first=False):
                act.wait_ge(v_done, n)
                if not first:
                    act.wait_ge(pv_done, TPB * (n - 2) + 2 * (half + 1))
                tiles = slice(2 * half, 2 * half + 2)
                v = bank[:, :].rearrange("k (t h d) -> k t h d", t=TPB, d=HD)
                for j in range(NJ):
                    r = slice(j * BLK, (j + 1) * BLK)
                    nc.scalar.copy(VD[r, tiles, 1, :, j, 0:HD], v[r, tiles, :, :])
                    if j > 0:
                        nc.scalar.copy(VD[r, tiles, 0, :, j, 0:HD], v[(j - 1) * BLK : j * BLK, tiles, :, :])
                behind = slice(max(2 * half, 1), 2 * half + 2)
                nc.scalar.copy(
                    VD[0:BLK, behind, 0, :, 0, 0:HD], v[P - BLK :, max(2 * half - 1, 0) : 2 * half + 1, :, :]
                ).then_inc(v_ready, 1)

            def exponentials(b, k, first=False):
                act.wait_ge(sub_done, b * TPB + (k + 1))
                if k >= 2 or not first:
                    act.wait_ge(pt_done, b * TPB + (k - 1))
                nc.scalar.activation(
                    Pr[:, k % 2, :], Sd[:, k % 2, :, :].rearrange("q h k -> q (h k)"), ACT.Exp, scale=SCALE
                ).then_inc(exp_done, 1)

            def normalise(b, first=False):
                if not first:
                    act.wait_ge(xt_done, b)
                for k in range(TPB):
                    at = bass.ds(b * TPB + k, 1)
                    last = nc.scalar.activation(
                        xn[:, k : k + 1, :], x_all[:, at, :], ACT.Identity, bias=ln_b[:, at], scale=rstd[:, at]
                    )
                last.then_inc(norm_done, 1)

            act.wait_ge(bqkv_in, 16)
            act.wait_ge(shift_ready, 1)
            normalise(0, first=True)
            evict_xnT(1, first=True)
            act.wait_ge(bk_of_ready, 1)
            evict_k(1, 0)
            act.wait_ge(filled, after["VD"])
            evict_v(1, 0, psA, first=True)
            deviations(TPB, NT, 2)
            evict_v(1, 1, psA, first=True)
            exponentials(0, 0, first=True)
            act.wait_ge(shift_ready, 2)
            normalise(1)
            evict_xnT(2)
            act.wait_ge(filled, after["Qx 1"])

            def batch(b, odd, first=False, qkv=True, xt=True):
                if qkv:
                    if not first:
                        act.wait_ge(s_done, b * TPB)
                    evict_q(b + 2, 1 - odd)
                exponentials(b, 1, first=first)
                if qkv:
                    evict_k(b + 2, 1 - odd)
                exponentials(b, 2)
                if xt:
                    normalise(b + 2)
                exponentials(b, 3)
                if qkv:
                    evict_v(b + 2, 0)
                if xt:
                    evict_xnT(b + 3)
                if qkv:
                    exponentials(b + 1, 0)
                    evict_v(b + 2, 1)

            batch(0, 0, first=True)
            with act.Fori(1, B - 3, 2) as b:
                batch(b, 1)
                batch(b + 1, 0)
            batch(B - 3, 1)
            batch(B - 2, 0, xt=False)
            batch(B - 1, 1, qkv=False, xt=False)

            deviations(0, NT - TPB, 3)

            def turned_batch(b):
                act.wait_ge(rows_turned, b + 1)
                bank = (psA, psB)[b % 2]
                nc.scalar.copy(xn2T[:, b * T : (b + 1) * T], bank[:, :]).then_inc(xn2T_ready, 1)
                nc.scalar.copy(xn2T_hi[:, b * T : (b + 1) * T], bank[:, :]).then_inc(xn2T_hi_ready, 1)

            def shared_silu(b, c, first=False):
                act.wait_ge(g_done, b * NC + (c + 1))
                if c >= 2 or not first:
                    act.wait_ge(h_done, b * NC + (c - 1))
                nc.scalar.activation(sg[:, c % 2, :], psS[:, c % 2, 512:], ACT.Silu).then_inc(silu_done, 1)

            turned_batch(0)
            deviations(NT - TPB, NT, 4)
            turned_batch(1)
            shared_silu(0, 0, first=True)
            for c in range(1, NC):
                shared_silu(0, c, first=True)
                turned_batch(2 * c)
                turned_batch(2 * c + 1)
            for c in range(NC):
                shared_silu(1, c)
            shared_silu(2, 0)
            act.wait_ge(logit_d_ready, 1)
            nc.scalar.activation(logit_e[:, :, :], logit_d[:, :, :], ACT.Exp).then_inc(logit_e_ready, 1)
            for c in range(1, NC):
                shared_silu(2, c)
            with act.Fori(3, B - 1) as b:
                for c in range(NC):
                    shared_silu(b, c)

            def turned_rows(i, r):
                act.wait_ge(xsT_done, i + 1)
                nc.scalar.copy(xsT[:, r % 2, 0, :], psA[:, 0:P]).then_inc(xsT_ready, 1)

            def expert_step(s, r, ug=True, ht=True, xt=True):
                if xt:
                    turned_rows(s + 1, r + 1)
                if ht:
                    act.wait_ge(ehT_done, s)
                    nc.scalar.copy(hsT[:, (r + 1) % 2, :], psO[:, (r + 1) % 2, :]).then_inc(ehT_ready, 1)
                if ug:
                    act.wait_ge(eg_done, s + 1)
                    if r >= 2:
                        act.wait_ge(eh_done, s - 1)
                    else:
                        act.wait_ge(h_done, B * NC - 1 + r)
                    nc.scalar.activation(sg[:, r % 2, :], psS[:, r % 2, 512:], ACT.Silu).then_inc(esilu_done, 1)

            for c in range(NC - 1):
                shared_silu(B - 1, c)
            turned_rows(0, 0)
            shared_silu(B - 1, NC - 1)
            expert_step(0, 0, ht=False)
            for s in range(1, RING + 2):
                expert_step(s, s)
            with act.Fori(RING + 2, MT - RING, RING) as s:
                for r in range(RING):
                    expert_step(s + r, 2 + r)
            expert_step(MT - 1, MT - 1, xt=False)
            expert_step(MT, MT, ug=False, xt=False)

        @block.vector
        def _(dve):
            step = [0]

            def then(ins):
                step[0] += 1
                ins.then_inc(ln_step, 1)
                dve.wait_ge(ln_step, step[0])

            def ln_moments(lo, hi):
                t = slice(lo, hi)
                me, mo = stats[:, t, 1], stats[:, t, 4]
                then(nc.vector.tensor_tensor(ln_a[:, t], me, mo, ALU.subtract))
                then(nc.vector.tensor_tensor(mean[:, t], me, mo, ALU.add))
                then(nc.vector.tensor_scalar(mean[:, t], mean[:, t], 0.5, None, ALU.mult))
                then(nc.vector.tensor_tensor(ln_a[:, t], ln_a[:, t], ln_a[:, t], ALU.mult))
                then(nc.vector.tensor_scalar(ln_a[:, t], ln_a[:, t], 0.25, EPS, ALU.mult, ALU.add))
                then(nc.vector.tensor_tensor(ln_b[:, t], stats[:, t, 2], stats[:, t, 5], ALU.add))
                nc.vector.scalar_tensor_tensor(
                    out=ln_ve[:, t], in0=ln_b[:, t], scalar=1.0 / D, in1=ln_a[:, t], op0=ALU.mult, op1=ALU.add
                ).then_inc(ln_ve_ready, 1)

            def ln_rstd(lo, hi, n):
                t = slice(lo, hi)
                dve.wait_ge(ln_ve_ready, n)
                dve.wait_ge(ln_sd_ready, n)
                then(nc.vector.reciprocal(rstd[:, t], ln_sd[:, t]))
                then(nc.vector.tensor_tensor(ln_a[:, t], rstd[:, t], rstd[:, t], ALU.mult))
                then(nc.vector.tensor_tensor(ln_a[:, t], ln_a[:, t], ln_ve[:, t], ALU.mult))
                then(nc.vector.tensor_scalar(ln_a[:, t], ln_a[:, t], -0.5, 1.5, ALU.mult, ALU.add))
                then(nc.vector.tensor_tensor(rstd[:, t], rstd[:, t], ln_a[:, t], ALU.mult))

            def ln_shift(lo, hi):
                t = slice(lo, hi)
                nc.vector.scalar_tensor_tensor(
                    out=ln_b[:, t], in0=mean[:, t], scalar=-1.0, in1=rstd[:, t], op0=ALU.mult, op1=ALU.mult
                ).then_inc(shift_ready, 1)

            def input_stats(lo, hi, n):
                for b in range(lo, hi):
                    dve.wait_ge(x_in[b], 16)
                    for g in range(b * TPB, (b + 1) * TPB):
                        last = nc.vector.bn_stats(stats[:, g, :], x_all[:, g, :])
                last.then_inc(stats1_done, 1)
                dve.wait_ge(stats1_done, n)

            def find_max(b, k):
                s = psS[:, k % 2, :].rearrange("q (h k) -> q h k", k=KEYS)
                dve.wait_ge(s_done, b * TPB + (k + 1))
                nc.vector.tensor_reduce(row_max[:, k % 2, :], s, AX.X, ALU.max).then_inc(max_done, 1)

            def subtract_max(b, k, first=False):
                s = psS[:, k % 2, :].rearrange("q (h k) -> q h k", k=KEYS)
                dve.wait_ge(max_done, b * TPB + (k + 1))
                if k >= 2 or not first:
                    dve.wait_ge(exp_done, b * TPB + (k - 1))
                nc.vector.tensor_tensor(
                    Sd[:, k % 2, :, :], s, row_max[:, k % 2, :].unsqueeze(2).to_broadcast([P, NH, KEYS]), ALU.subtract
                ).then_inc(sub_done, 1)

            nc.vector.memset(Kx[:, :, :, 0:BLK], 0.0)
            nc.vector.memset(Qx[:, 0, :, :], 0.0).then_inc(zeros_ready, 1)
            input_stats(0, 1, 1)
            ln_moments(0, TPB)
            dve.wait_ge(filled, after["ident"])
            nc.vector.tensor_reduce(
                head_of[:, :], ident[:, :].rearrange("p (g h d) -> p h g d", g=NG, d=HD), AX.XY, ALU.add
            ).then_inc(head_of_ready, 1)
            ln_rstd(0, TPB, 1)
            ln_shift(0, TPB)
            dve.wait_ge(head_of_ready, 1)
            dve.wait_ge(bqkv_in, 16)
            nc.vector.tensor_scalar(bk_of[:, :], head_of[:, :], bqkv_sb[:, 1:2], None, ALU.mult).then_inc(bk_of_ready, 1)
            nc.vector.tensor_scalar(bv_wide[:, :], ones[:, 0:P], bqkv_sb[:, 2:3], None, ALU.mult).then_inc(
                bv_wide_ready, 1
            )
            input_stats(1, B - 2, 2)
            dve.wait_ge(qk_done, 1)
            for g in range(NG):
                r = slice(g * BLK, (g + 1) * BLK)
                last = nc.vector.tensor_scalar(Qx[r, 0, g, :], psA[r, :], bqkv_sb[r, 0:1], None, ALU.add)
            last.then_inc(q_ready, 1)
            input_stats(B - 2, B, 3)
            ln_moments(TPB, NT)
            find_max(0, 0)
            ln_rstd(TPB, NT, 2)
            subtract_max(0, 0, first=True)
            ln_shift(TPB, NT)
            dve.wait_ge(bias_mm, 1)
            nc.vector.tensor_copy(attn_bias[:, 0, :], psO[:, 0, 0:D]).then_inc(bias_ready, 1)
            dve.wait_ge(bias_ready, 1)
            for bank in range(2):
                nc.vector.memset(esum[:, 0:1], 0.0).then_inc(o_free, 1)
                dve.wait_ge(o_free, bank + 1)

            def turn_probs(b, k, first=False):
                dve.wait_ge(exp_done, b * TPB + (k + 1))
                if k >= 2 or not first:
                    dve.wait_ge(pv_done, b * TPB + (k - 1))
                nc.vector.transpose(PT[:, k % 2, :], Pr[:, k % 2, :]).then_inc(pt_done, 1)

            def heads_sums(b, k):
                dve.wait_ge(pv_done, b * TPB + (k + 1))
                o = psO[:, k % 2, 0 : NH * VW].rearrange("q (h j v) -> q h j v", j=NJ, v=VW)
                r = rden[:, k % 2, :].rearrange("q (h j) -> q h j", j=NJ)
                nc.vector.reciprocal(r, o[:, :, :, HD]).then_inc(rden_done, 1)

            def divide_heads(b, k):
                o = psO[:, k % 2, 0 : NH * VW].rearrange("q (h j v) -> q h j v", j=NJ, v=VW)
                r = rden[:, k % 2, :].rearrange("q (h j) -> q h j", j=NJ)
                dve.wait_ge(rden_done, b * TPB + (k + 1))
                nc.vector.tensor_tensor(
                    On[:, k % 2, :].rearrange("q (j h d) -> q h j d", j=NJ, d=HD), o[:, :, :, 0:HD],
                    r.unsqueeze(3).to_broadcast([P, NH // NJ, NJ, HD]), ALU.mult,
                ).then_inc(on_done, 1)

            def turn_heads(b, k):
                dve.wait_ge(on_done, b * TPB + (k + 1))
                nc.vector.transpose(OT[:, k % 2, :], On[:, k % 2, :]).then_inc(ot_done, 1)

            def residual(b, k):
                dve.wait_ge(op_done, b * TPB + (k + 1))
                if k == 0:
                    dve.wait_ge(xb_done, b + 1)
                xk = x_all[:, bass.ds(b * TPB + k, 1), :]
                nc.vector.tensor_tensor(
                    xk, xk, psO[:, k % 2, OPC : OPC + D].unsqueeze(1), ALU.add
                ).then_inc(o_free, 1)

            def moments(b, k):
                at = bass.ds(b * TPB + k, 1)
                dve.wait_ge(o_free, b * TPB + (2 + k + 1))
                nc.vector.bn_stats(
                    stats[:, at, :].rearrange("p a s -> p (a s)"), x_all[:, at, :].rearrange("p a d -> p (a d)")
                ).then_inc(st2_done, 1)

            def tile(b, k, first=False, last=False):
                then_b, then_k = (b, k + 1) if k + 1 < TPB else (b + 1, 0)
                after_b, after_k = (b, k + 2) if k + 2 < TPB else (b + 1, k + 2 - TPB)
                before_b, before_k = (b, k - 1) if k > 0 else (b - 1, TPB - 1)
                if last and k + 2 >= TPB:
                    after_b = None
                last = last and k + 1 == TPB
                turn_probs(b, k, first=first)
                if not last:
                    subtract_max(then_b, then_k, first=first)
                if k > 0 or not first:
                    residual(before_b, before_k)
                if last:
                    dve.wait_ge(st2_done, NT - TPB)
                    ln_moments(0, NT - TPB)
                if after_b is not None:
                    find_max(after_b, after_k)
                heads_sums(b, k)
                if k > 0 or not first:
                    moments(before_b, before_k)
                divide_heads(b, k)
                turn_heads(b, k)

            def batch(b, first=False, last=False):
                for k in range(TPB):
                    tile(b, k, first=first, last=last)

            find_max(0, 1)
            batch(0, first=True)
            with dve.Fori(1, B - 1, 2) as b:
                batch(b)
                batch(b + 1)
            batch(B - 1, last=True)
            ln_rstd(0, NT - TPB, 3)
            residual(B - 1, TPB - 1)
            moments(B - 1, TPB - 1)

            dve.wait_ge(consts_ready, 1)

            def normalise_rows(b):
                for g in range(b * TPB, (b + 1) * TPB):
                    last = nc.vector.tensor_scalar(
                        rows[:, g, 0, 0:D], x_all[:, g, :], mean[:, g : g + 1], rstd[:, g : g + 1],
                        ALU.subtract, ALU.mult,
                    )
                last.then_inc(rows_ready, 1)

            def low_parts(b):
                dve.wait_ge(xn2T_hi_ready, b + 1)
                dve.wait_ge(logits_done, (b + 1) * TPB)
                t = slice(b * T, (b + 1) * T)
                nc.vector.tensor_tensor(xn2T_lo[:, t], xn2T[:, t], xn2T_hi[:, t].bitcast(f32), ALU.subtract).then_inc(
                    xn2T_lo_ready, 1
                )

            def shared_hidden(b, c, first=False):
                dve.wait_ge(u_done, b * NC + (c + 1))
                dve.wait_ge(silu_done, b * NC + (c + 1))
                if not first:
                    dve.wait_ge(down_done, b)
                nc.vector.tensor_tensor(hT[:, c, :], psS[:, c % 2, 0:512], sg[:, c % 2, :], ALU.mult).then_inc(h_done, 1)

            def shared_residual(b):
                dve.wait_ge(down_done, b + 1)
                xb = x_all[:, bass.ds(b * TPB, TPB), :]
                nc.vector.tensor_tensor(
                    xb, xb, psO[:, 1, :].rearrange("p (k d) -> p k d", d=D), ALU.add
                ).then_inc(base_done, 1)

            def wide(a):
                return a.unsqueeze(2).to_broadcast([P, NT, E])

            def find_largest():
                logits = psO[:, 0, 0 : NT * E].rearrange("p (g e) -> p g e", e=E)
                dve.wait_ge(logits_done, NT)
                then(nc.vector.tensor_reduce(top[:, :], logits, AX.X, ALU.max))
                nc.vector.tensor_tensor(logit_d[:, :, :], logits, wide(top[:, :]), ALU.subtract).then_inc(logit_d_ready, 1)
                dve.wait_ge(logit_d_ready, 1)

            def choose_first():
                then(nc.vector.scalar_tensor_tensor(
                    out=chosen[:, :, :], in0=logit_d[:, :, :], scalar=0.0,
                    in1=rank_of[:, :].unsqueeze(1).to_broadcast([P, NT, E]), op0=ALU.is_ge, op1=ALU.mult,
                ))
                then(nc.vector.tensor_reduce(best[:, :], chosen[:, :, :], AX.X, ALU.max))

            def mark_choices():
                then(nc.vector.tensor_tensor(chosen[:, :, :], chosen[:, :, :], wide(best[:, :]), ALU.is_equal))
                nc.vector.tensor_copy(chosen_h[:, :, :].rearrange("p e g -> p g e"), chosen[:, :, :]).then_inc(chosen_ready, 1)

            def gates():
                then(nc.vector.tensor_scalar(has_expert[:, :], chosen[:, :, NE], -ALPHA, ALPHA, ALU.mult, ALU.add))
                dve.wait_ge(logit_e_ready, 1)
                then(nc.vector.tensor_reduce(esum[:, :], logit_e[:, :, :], AX.X, ALU.add))
                then(nc.vector.reciprocal(esum[:, :], esum[:, :]))
                nc.vector.tensor_tensor(rows[:, :, 0, GATE], esum[:, :], has_expert[:, :], ALU.mult).then_inc(gates_ready, 1)

            flat = "p e g -> p (e g)"

            def count_choices():
                in_tile = psB[:, 0 : E * NT]
                dve.wait_ge(counted, 1)
                then(nc.vector.tensor_tensor_scan(
                    seen[:, :, :].rearrange(flat), ones[:, :], in_tile, 0.0, ALU.mult, ALU.add
                ))
                then(nc.vector.tensor_tensor(
                    pos3[:, :, :].rearrange(flat), seen[:, :, :].rearrange(flat), in_tile, ALU.subtract
                ))

            def count_tiles():
                then(nc.vector.tensor_tensor(count[:, :], seen[:, :, NT - 1], pos3[:, :, 0], ALU.subtract))
                then(nc.vector.tensor_tensor(
                    full[:, :, :], count[:, :].unsqueeze(2).to_broadcast([P, E, NT]),
                    row_no[:, :].unsqueeze(1).to_broadcast([P, E, NT]), ALU.is_gt,
                ))
                then(nc.vector.tensor_reduce(tiles_of[:, :], full[:, :, :], AX.X, ALU.add))

            def place_choices():
                then(nc.vector.tensor_tensor_scan(tiles_end[:, :], ones[:, 0:E], tiles_of[:, :], 0.0, ALU.mult, ALU.add))
                then(nc.vector.tensor_tensor(shift[:, :], tiles_end[:, :], tiles_of[:, :], ALU.subtract))
                then(nc.vector.scalar_tensor_tensor(
                    out=shift[:, :], in0=shift[:, :], scalar=float(P), in1=pos3[:, :, 0], op0=ALU.mult, op1=ALU.subtract
                ))

            def place_in_choices():
                within = psA[:, 0 : E * NT].rearrange("p (e g) -> p e g", e=E)
                then(nc.vector.tensor_tensor(pos3[:, :, :], pos3[:, :, :], within, ALU.add))
                then(nc.vector.tensor_tensor(
                    pos3[:, :, :], pos3[:, :, :], shift[:, :].unsqueeze(2).to_broadcast([P, E, NT]), ALU.add
                ))

            def place_tokens():
                then(nc.vector.tensor_tensor(
                    pos3[:, :, :], pos3[:, :, :], chosen[:, :, :].rearrange("p g e -> p e g"), ALU.mult
                ))
                then(nc.vector.tensor_reduce(pos[:, :], pos3[:, :, :].rearrange("p e g -> p g e"), AX.X, ALU.add))
                late = pos[:, (B - LATE) * TPB :]
                then(nc.vector.tensor_scalar(half_pos[:, 0, :], late, 2.0, None, ALU.mult))
                then(nc.vector.tensor_scalar(half_pos[:, 1, :], late, 2.0, 1.0, ALU.mult, ALU.add))
                then(nc.vector.tensor_copy(half_pos_u[:, :, :], half_pos[:, :, :]))
                nc.vector.tensor_copy(pos_u[:, :], pos[:, :]).then_inc(pos_ready, 1)

            def experts_of_tiles():
                then(nc.vector.tensor_tensor(
                    past[:, :, :], tile_no[:, :].unsqueeze(2).to_broadcast([P, MT, NE]),
                    tiles_end[:, 0:NE].unsqueeze(1).to_broadcast([P, MT, NE]), ALU.is_ge,
                ))
                then(nc.vector.tensor_reduce(tile_e[:, :], past[:, :, :], AX.X, ALU.add))
                then(nc.vector.tensor_scalar(
                    tile_e[:, :], tile_e[:, :], float(NE - 1), float(HID), ALU.min, ALU.mult
                ))
                nc.vector.tensor_copy(tile_at[:, :], tile_e[:, :]).then_inc(tile_at_ready, 1)

            def expert_low_parts(i, r):
                dve.wait_ge(xsT_ready, i + 1)
                hi = xsT[:, r % 2, 0, :].bitcast(f32)
                nc.vector.tensor_tensor(xsT[:, r % 2, 1, :], psA[:, 0:P], hi, ALU.subtract).then_inc(xsT_lo_ready, 1)

            normalise_rows(0)
            normalise_rows(1)
            dve.wait_ge(st2_done, NT)
            ln_moments(NT - TPB, NT)
            low_parts(0)
            ln_rstd(NT - TPB, NT, 4)
            normalise_rows(2)
            shared_hidden(0, 0, first=True)
            normalise_rows(3)
            for c in range(1, NC):
                shared_hidden(0, c, first=True)
                if c < NC - 1:
                    normalise_rows(2 * c + 2)
                    normalise_rows(2 * c + 3)
                low_parts(2 * c - 1)
                low_parts(2 * c)
            low_parts(B - 1)
            find_largest()
            choose_first()
            shared_hidden(1, 0)
            shared_residual(0)
            shared_hidden(1, 1)
            mark_choices()
            shared_hidden(1, 2)
            shared_hidden(1, 3)
            count_choices()
            count_tiles()
            place_choices()
            shared_hidden(2, 0)
            shared_residual(1)
            shared_hidden(2, 1)
            place_in_choices()
            shared_hidden(2, 2)
            shared_hidden(2, 3)
            gates()
            place_tokens()
            experts_of_tiles()
            shared_hidden(3, 0)
            shared_residual(2)
            shared_hidden(3, 1)
            shared_hidden(3, 2)
            shared_hidden(3, 3)
            with dve.Fori(4, B - 1) as b:
                shared_hidden(b, 0)
                shared_residual(b - 1)
                for c in range(1, NC):
                    shared_hidden(b, c)
            shared_hidden(B - 1, 0)
            shared_residual(B - 2)
            for c in range(1, NC - 1):
                shared_hidden(B - 1, c)
            expert_low_parts(0, 0)
            shared_hidden(B - 1, NC - 1)
            for k in range(TPB):
                xk = x_all[:, (B - 1) * TPB + k, :]
                dve.wait_ge(down_done, B - 1 + (k + 1))
                nc.vector.tensor_tensor(xk, xk, psO[:, k % 2, 0:D], ALU.add).then_inc(base_done, 1)

            def expert_step(s, r, ug=True, down=True, xt=True):
                if down:
                    q = (r - 2) % RING
                    dve.wait_ge(ey_done, s - 1)
                    dve.wait_ge(base_in[q], loads(s - 2, r - 2))
                    nc.vector.tensor_tensor(y[:, q, :], psB[:, 0:D], base[:, q, :], ALU.add).then_inc(y_ready, 1)
                if xt:
                    expert_low_parts(s + 1, r + 1)
                if ug:
                    q = r % RING
                    dve.wait_ge(xs_in[q], loads(s, r))
                    if r >= RING:
                        dve.wait_ge(written[q], loads(s, r) - 16)
                    nc.vector.tensor_copy(tok_u[:, q : q + 1], xs[:, q, TOKEN : TOKEN + 1])
                    dve.wait_ge(eu_done, s + 1)
                    dve.wait_ge(esilu_done, s + 1)
                    if r >= 2:
                        dve.wait_ge(ehT_done, s - 1)
                    for half, done in enumerate((eh_half, eh_done)):
                        h = slice(half * HID // 2, (half + 1) * HID // 2)
                        nc.vector.scalar_tensor_tensor(
                            out=hs[:, r % 2, h], in0=psS[:, r % 2, h], scalar=xs[:, q, GATE : GATE + 1],
                            in1=sg[:, r % 2, h], op0=ALU.mult, op1=ALU.mult,
                        ).then_inc(done, 1)

            for s in range(RING + 2):
                expert_step(s, s, down=s >= 2)
            with dve.Fori(RING + 2, MT - RING, RING) as s:
                for r in range(RING):
                    expert_step(s + r, RING + 2 + r)
            expert_step(MT - 1, MT - 1, xt=False)
            expert_step(MT, MT, ug=False, xt=False)
            expert_step(MT + 1, MT + 1, ug=False, xt=False)

        @block.tensor
        def _(pe):
            mm = nc.tensor.matmul

            def turn_x(n, first=False):
                pe.wait_ge(norm_done, n)
                if not first:
                    pe.wait_ge(q_ready, n - 1)
                for k in range(TPB):
                    last = nc.tensor.transpose(psA[:, k * P : (k + 1) * P], xn[:, k, :], ident[:, :])
                last.then_inc(xt_done, 1)

            def queries_keys(n, first=False):
                pe.wait_ge(xnT_ready, n)
                mm(psA[:, :], wqkv_sb[:, 0:D], xnT[:, :], start=True, stop=True).then_inc(qk_done, 1)
                if not first:
                    pe.wait_ge(v_ready, 2 * (n - 1))
                mm(psB[:, :], wqkv_sb[:, D : 2 * D], xnT[:, :], start=True, stop=True).then_inc(qk_done, 1)

            def values(bank):
                for k in range(TPB):
                    w = slice(k * P, (k + 1) * P)
                    last = mm(bank[:, w], xnT[:, w], wqkv_sb[:, 2 * D :], start=True, stop=True)
                last.then_inc(v_done, 1)

            def scores(b, odd, k, first=False):
                if k == 0:
                    pe.wait_ge(q_ready, b + 1)
                    pe.wait_ge(k_ready, b + 1)
                if k >= 2 or not first:
                    pe.wait_ge(sub_done, b * TPB + (k - 1))
                variant = 0 if k == 0 else 1
                for half in range(2):
                    s = psS[:, k % 2, 512 * half : 512 * (half + 1)]
                    mm(s, ident_h[:, :], mask_h[:, variant, :, :], start=True, stop=False, skip_group_check=True)
                    for gg in range(HPB // HPG):
                        g = half * (HPB // HPG) + gg
                        for j in range(NJ):
                            at = k * P + j * BLK
                            last = mm(
                                s[j * BLK : (j + 1) * BLK, gg * HPG * KEYS : (gg + 1) * HPG * KEYS],
                                Qx[:, odd, g, at : at + BLK], Kx[:, odd, :, at : at + KEYS],
                                start=False, stop=True, skip_group_check=True,
                            )
                last.then_inc(s_done, 1)

            def weigh_values(b, k):
                pe.wait_ge(pt_done, b * TPB + (k + 1))
                pe.wait_ge(o_free, b * TPB + (k + 1))
                if k % 2 == 0:
                    pe.wait_ge(v_ready, 2 * b + (k // 2 + 1))
                for hh in range(NH // NJ):
                    for c in range(2):
                        for g in range(NJ):
                            h = g * (NH // NJ) + hh
                            last = mm(
                                psO[g * BLK : (g + 1) * BLK, k % 2, hh * NJ * VW : (hh + 1) * NJ * VW],
                                PT[:, k % 2, (2 * h + c) * BLK : (2 * h + c + 1) * BLK],
                                VD[:, k, c, h, :, :].rearrange("k j v -> k (j v)"),
                                start=(c == 0), stop=(c == 1),
                            )
                last.then_inc(pv_done, 1)

            def project(b, k):
                pe.wait_ge(ot_done, b * TPB + (k + 1))
                mm(psO[:, k % 2, OPC : OPC + D], OT[:, k % 2, :], wout_sb[:, :], start=True, stop=True).then_inc(
                    op_done, 1
                )

            def keep_warm(bank, n):
                for _ in range(n):
                    mm(bank, ones_h[:, :], ones_h[:, :], start=True, stop=True)

            pe.wait_ge(filled, after["ones_h"])
            keep_warm(psS[:, 0, 0:P], WARM)
            pe.wait_ge(filled, after["ident"])
            turn_x(1, first=True)
            pe.wait_ge(wqkv_in, 16)
            pe.wait_ge(zeros_ready, 1)
            queries_keys(1, first=True)
            pe.wait_ge(bv_wide_ready, 1)
            pe.wait_ge(wout_in, 16)
            pe.wait_ge(bout_in, 16)
            mm(psO[:, 0, 0:D], bv_wide[:, :], wout_sb[:, :], start=True, stop=False)
            mm(psO[:, 0, 0:D], ones[0:1, 0:P], bout_sb[0:1, :], start=False, stop=True).then_inc(bias_mm, 1)
            pe.wait_ge(q_ready, 1)
            values(psA)
            pe.wait_ge(filled, after["masks"])
            scores(0, 0, 0, first=True)
            scores(0, 0, 1, first=True)
            scores(0, 0, 2)
            pe.wait_ge(v_ready, 2)
            turn_x(2)

            def batch(b, odd, qkv=True, xt=True):
                if qkv:
                    queries_keys(b + 2)
                weigh_values(b, 0)
                if not qkv:
                    keep_warm(psA[:, 0:P], WARM_LAST[0])
                scores(b, odd, 3)
                project(b, 0)
                weigh_values(b, 1)
                if not qkv:
                    keep_warm(psA[:, 0:P], WARM_LAST[1])
                if qkv:
                    scores(b + 1, 1 - odd, 0)
                project(b, 1)
                if qkv:
                    values(psB)
                weigh_values(b, 2)
                if not qkv:
                    keep_warm(psA[:, 0:P], WARM_LAST[2])
                if qkv:
                    scores(b + 1, 1 - odd, 1)
                project(b, 2)
                if xt:
                    turn_x(b + 3)
                weigh_values(b, 3)
                if not qkv:
                    keep_warm(psA[:, 0:P], WARM_LAST[3])
                if qkv:
                    scores(b + 1, 1 - odd, 2)
                project(b, 3)

            batch(0, 0)
            with pe.Fori(1, B - 3, 2) as b:
                batch(b, 1)
                batch(b + 1, 0)
            batch(B - 3, 1)
            batch(B - 2, 0, xt=False)
            batch(B - 1, 1, qkv=False, xt=False)

            def turn_rows(b):
                pe.wait_ge(rows_ready, b + 1)
                if b >= 2:
                    pe.wait_ge(xn2T_hi_ready, b - 1)
                for k in range(TPB):
                    bank = (psA, psB)[b % 2]
                    last = nc.tensor.transpose(bank[:, k * P : (k + 1) * P], rows[:, b * TPB + k, 0, 0:D], ident[:, :])
                last.then_inc(rows_turned, 1)

            def route(b):
                pe.wait_ge(xn2T_ready, b + 1)
                for g in range(b * TPB, (b + 1) * TPB):
                    mm(
                        psO[:, 0, g * E : (g + 1) * E], xn2T[:, g * P : (g + 1) * P], wr_sb[:, :], start=True, stop=True
                    ).then_inc(logits_done, 1)

            def rank_tokens():
                pe.wait_ge(consts_ready, 1)
                pe.wait_ge(chosen_ready, 1)
                ch = chosen_h[:, :, :].rearrange("p e g -> p (e g)")
                mm(psA[:, 0 : E * NT], before_h[:, :], ch, start=True, stop=True)
                mm(psB[:, 0 : E * NT], ones_h[:, :], ch, start=True, stop=True).then_inc(counted, 1)

            def shared_up(b, c, first=False):
                if c >= 2 or not first:
                    pe.wait_ge(h_done, b * NC + (c - 1))
                if c == 0:
                    pe.wait_ge(xn2T_lo_ready, b + 1)
                t, w = bass.ds(b * T, T), slice(SHARED * HID + c * P, SHARED * HID + (c + 1) * P)
                for bank, hi, lo, done in (
                    (psS[:, c % 2, 512:], gate_hi[:, w], gate_lo[:, w], g_done),
                    (psS[:, c % 2, 0:512], up_hi[:, w], up_lo[:, w], u_done),
                ):
                    mm(bank, lo, xn2T_hi[:, t], start=True, stop=False)
                    mm(bank, hi, xn2T_lo[:, t], start=False, stop=False)
                    mm(bank, hi, xn2T_hi[:, t], start=False, stop=True).then_inc(done, 1)

            def shared_down(b, first=False):
                pe.wait_ge(h_done, b * NC + NC)
                if not first:
                    pe.wait_ge(base_done, b)
                for k in range(TPB):
                    for c in range(NC):
                        last = mm(
                            psO[:, 1, k * D : (k + 1) * D], hT[:, c, k * P : (k + 1) * P],
                            down_sb[:, SHARED, c * D : (c + 1) * D], start=(c == 0), stop=(c == NC - 1),
                        )
                last.then_inc(down_done, 1)

            keep_warm(psA[:, 0:P], WARM_LAST[TPB])
            turn_rows(0)
            turn_rows(1)
            pe.wait_ge(wr_in, 16)
            route(0)
            pe.wait_ge(shared_split, 2)
            pe.wait_ge(shared_in[2], 16)
            shared_up(0, 0, first=True)
            for c in range(1, NC):
                shared_up(0, c, first=True)
                turn_rows(2 * c)
                route(2 * c - 1)
                turn_rows(2 * c + 1)
                route(2 * c)
            route(B - 1)
            shared_up(1, 0)
            shared_down(0, first=True)
            for c in range(1, NC):
                shared_up(1, c)
            rank_tokens()
            with pe.Fori(2, B - 1) as b:
                shared_up(b, 0)
                shared_down(b - 1)
                for c in range(1, NC):
                    shared_up(b, c)
            shared_up(B - 1, 0)
            shared_down(B - 2)
            for c in range(1, NC - 1):
                shared_up(B - 1, c)

            down_flat = down_sb[:, :, :].rearrange("p e h -> p (e h)")

            def expert_turn_rows(i, r):
                pe.wait_ge(xs_in[r % RING], loads(i, r))
                if r >= 1:
                    pe.wait_ge(xsT_lo_ready, i)
                nc.tensor.transpose(psA[:, 0:P], xs[:, r % RING, 0:D], ident[:, :]).then_inc(xsT_done, 1)

            def weights_of(i, n=1):
                _, starts = nc.values_load_multi_w_load_instructions(
                    tile_at[0:1, bass.ds(i, n)], engines=[mybir.EngineType.PE], min_val=0, max_val=(NE - 1) * HID
                )
                return list(starts)

            def expert_product(s, r, start, half, hi, lo, done):
                w = bass.ds(start, HID)
                x_hi, x_lo = xsT[:, r % 2, 0, :], xsT[:, r % 2, 1, :]
                pe.wait_ge(xsT_lo_ready, s + 1)
                if r >= 2:
                    pe.wait_ge(eh_done, s - 1)
                else:
                    pe.wait_ge(h_done, B * NC - 1 + r)
                bank = psS[:, r % 2, half * 512 : (half + 1) * 512]
                mm(bank, x_lo, hi[:, w], start=True, stop=False)
                mm(bank, x_hi, lo[:, w], start=False, stop=False)
                mm(bank, x_hi, hi[:, w], start=False, stop=True).then_inc(done, 1)

            def expert_gate(s, r, start):
                expert_product(s, r, start, 1, gate_hi, gate_lo, eg_done)

            def expert_up(s, r, start):
                expert_product(s, r, start, 0, up_hi, up_lo, eu_done)

            def expert_step(s, r, at, ug=True, ht=True, xt=True, down=True, fetch=()):
                if down:
                    pe.wait_ge(ehT_ready, s - 1)
                    if r >= 3:
                        pe.wait_ge(y_ready, s - 2)
                    for c in range(NC):
                        last = mm(
                            psB[:, 0:D], hsT[:, r % 2, c * P : (c + 1) * P], down_flat[:, bass.ds(at[r - 2] + c * D, D)],
                            start=(c == 0), stop=(c == NC - 1),
                        )
                    last.then_inc(ey_done, 1)
                if xt:
                    expert_turn_rows(s + 1, r + 1)
                for n in fetch:
                    [at[r + n]] = weights_of(s + n)
                if ht:
                    pe.wait_ge(eh_half, s)
                    for c in range(NC):
                        if c == NC // 2:
                            pe.wait_ge(eh_done, s)
                        hidden = slice(c * P, (c + 1) * P)
                        last = nc.tensor.transpose(psO[:, (r + 1) % 2, hidden], hs[:, (r + 1) % 2, hidden], ident[:, :])
                    last.then_inc(ehT_done, 1)
                if ug:
                    expert_gate(s, r, at[r])
                    expert_up(s, r, at[r])

            pe.wait_ge(experts_split, 2)
            pe.wait_ge(experts_in[2], 16)
            pe.wait_ge(tile_at_ready, 1)
            expert_turn_rows(0, 0)
            shared_up(B - 1, NC - 1)
            first = RING + 2
            at = dict(enumerate(weights_of(0)))
            expert_gate(0, 0, at[0])
            pe.wait_ge(h_done, B * NC)
            for k in range(TPB):
                pe.wait_ge(base_done, B - 1 + max(k - 1, 0))
                for c in range(NC):
                    last = mm(
                        psO[:, k % 2, 0:D], hT[:, c, k * P : (k + 1) * P], down_sb[:, SHARED, c * D : (c + 1) * D],
                        start=(c == 0), stop=(c == NC - 1),
                    )
                last.then_inc(down_done, 1)
            expert_up(0, 0, at[0])
            expert_step(0, 0, at, ug=False, ht=False, down=False, fetch=(1,))
            for s in range(1, first):
                expert_step(s, s, at, down=s >= 2, fetch=(1,) if s < first - 1 else ())
            turns = 4 * RING
            with pe.Fori(first, MT - 1 - turns + 1, turns) as s:
                at = dict(zip(range(first - 2, first + 1), weights_of(s - 2, 3)))
                for r in range(turns):
                    expert_step(s + r, first + r, at, fetch=(1,) if r < turns - 1 else ())
            at = dict(zip(range(MT - 3, MT), weights_of(MT - 3, 3)))
            expert_step(MT - 1, MT - 1, at, xt=False)
            expert_step(MT, MT, at, ug=False, xt=False)
            expert_step(MT + 1, MT + 1, at, ug=False, ht=False, xt=False)


_INS = [
    "L0_attn_x", "L0_attn_W_qkv", "L0_attn_b_qkv", "L0_attn_W_out", "L0_attn_b_out", "L0_ffn_w_router",
    "L0_ffn_w_up", "L0_ffn_w_gate", "L0_ffn_w_down", "L0_ffn_ws_up", "L0_ffn_ws_gate", "L0_ffn_ws_down",
]


def kernel(**inputs):
    import concourse.bacc as bacc
    import numpy as np
    from concourse.bass_utils import run_bass_kernel_spmd

    nc = bacc.Bacc("TRN2", target_bir_lowering=False, num_devices=1)
    arrays, args = {}, []
    for name in _INS:
        a = np.ascontiguousarray(inputs[name])
        arrays[f"in_{name}"] = a
        args.append(nc.dram_tensor(f"in_{name}", a.shape, mybir.dt.from_np(a.dtype), kind="ExternalInput").ap())
    x = arrays["in_L0_attn_x"]
    args.append(nc.dram_tensor("out", x.shape, mybir.dt.from_np(x.dtype), kind="ExternalOutput").ap())
    windowed_attention_top1_moe_kernel(nc, *args)
    return run_bass_kernel_spmd(nc, [arrays], core_ids=[0]).results[0]["out"]
```
